# Optimizing a Trainium2 kernel written in Bass

```python
import numpy as np
import jax
import jax.numpy as jnp

def _softmax(x, axis=-1):
    return jax.nn.softmax(x, axis=axis)

def _gelu(x):
    return jax.nn.gelu(x, approximate=True)

def _silu(x):
    return jax.nn.silu(x)

def _sigmoid(x):
    return jax.nn.sigmoid(x)

def _layernorm(x, axis=-1, eps=1e-05):
    m = jnp.mean(x, axis=axis, keepdims=True)
    v = jnp.var(x, axis=axis, keepdims=True)
    return (x - m) / jnp.sqrt(v + eps)

def _scatter_add(tgt, idx, src, axis=0):
    return tgt.at[idx].add(src)

def _segment_sum(src, seg, n):
    return jax.ops.segment_sum(src, seg, n)
kernel_name = 'mk_seq_preln_d2_jaxref_r8_e19150'

def setup_inputs(seed: int=0):
    np.random.seed(seed)
    _w = jnp.asarray

    def _L0_attn_setup():
        import jax, jax.numpy as jnp
        import numpy as np
        D_MODEL = 128
        N_HEADS = 16
        D_HEAD = D_MODEL // N_HEADS
        key = jax.random.key(seed)
        k1, k2, k3 = jax.random.split(key, 3)
        x = jax.random.normal(k1, (4, 256, D_MODEL), dtype=jnp.float32)
        s = 1.0 / np.sqrt(D_MODEL)
        W_qkv = jax.random.uniform(k2, (3 * D_MODEL, D_MODEL), dtype=jnp.float32, minval=-s, maxval=s)
        W_out = jax.random.uniform(k3, (D_MODEL, D_MODEL), dtype=jnp.float32, minval=-s, maxval=s)
        return {'x': x, 'W_qkv': W_qkv, 'W_out': W_out}
    _L0_attn_in = _L0_attn_setup()

    def _L0_ffn_setup():
        import jax, jax.numpy as jnp
        import numpy as np
        B, N, D = (4, 256, 128)
        SPARSITY = 0.01
        key = jax.random.key(seed)
        k1, k2, k3 = jax.random.split(key, 3)
        x = jax.random.normal(k1, (B, N, D), dtype=jnp.float32)
        spatial = jax.random.normal(k2, (D, D), dtype=jnp.float32) * 0.02
        freq = jnp.fft.fft(spatial, axis=-1)
        k = int(D * SPARSITY)
        mag = jnp.abs(freq)
        kth = jax.lax.top_k(mag, k)[0][:, -1:]
        w_sparse = jnp.where(mag >= kth, freq, 0.0 + 0j)
        bias = jax.random.normal(k3, (D,), dtype=jnp.float32) * 0.01
        return {'x': x, 'w_freq_real': jnp.real(w_sparse).astype(jnp.float32), 'w_freq_imag': jnp.imag(w_sparse).astype(jnp.float32), 'bias': bias}
    _L0_ffn_in = _L0_ffn_setup()

    def _L1_attn_setup():
        import jax, jax.numpy as jnp
        import numpy as np
        B, T, EMB, HEADS = (4, 256, 128, 16)
        CHUNK = EMB // HEADS
        key = jax.random.key(seed)
        kx, kq, kk, kv, ku = jax.random.split(key, 5)
        s = CHUNK ** (-0.5)
        return {'x': jax.random.normal(kx, (B, T, EMB), jnp.float32), 'Wq': jax.random.normal(kq, (CHUNK, CHUNK), jnp.float32) * s, 'Wk': jax.random.normal(kk, (CHUNK, CHUNK), jnp.float32) * s, 'Wv': jax.random.normal(kv, (CHUNK, CHUNK), jnp.float32) * s, 'Wu': jax.random.normal(ku, (EMB, EMB), jnp.float32) * EMB ** (-0.5), 'bu': jnp.zeros((EMB,), jnp.float32)}
    _L1_attn_in = _L1_attn_setup()

    def _L1_ffn_setup():
        import jax, jax.numpy as jnp
        import numpy as np
        B, S, D = (2, 128, 128)
        E, H, K, G = (8, 256, 2, 32)
        key = jax.random.key(seed)
        ks = jax.random.split(key, 5)
        return {'x': jax.random.normal(ks[0], (B, S, D), jnp.float32), 'wg1': jax.random.normal(ks[1], (D, G), jnp.float32) * 0.02, 'bg1': jnp.zeros((G,), jnp.float32), 'wg2': jax.random.normal(ks[2], (G, E), jnp.float32) * 0.02, 'w_in': jax.random.uniform(ks[3], (E, D, H), jnp.float32, -1.0 / D, 1.0 / D), 'w_out': jax.random.uniform(ks[4], (E, H, D), jnp.float32, -1.0 / H, 1.0 / H)}
    _L1_ffn_in = _L1_ffn_setup()
    _d = {'L0_attn_x': _L0_attn_in['x'], 'L0_attn_W_qkv': _L0_attn_in['W_qkv'], 'L0_attn_W_out': _L0_attn_in['W_out'], 'L0_ffn_w_freq_real': _L0_ffn_in['w_freq_real'], 'L0_ffn_w_freq_imag': _L0_ffn_in['w_freq_imag'], 'L0_ffn_bias': _L0_ffn_in['bias'], 'L1_attn_Wq': _L1_attn_in['Wq'], 'L1_attn_Wk': _L1_attn_in['Wk'], 'L1_attn_Wv': _L1_attn_in['Wv'], 'L1_attn_Wu': _L1_attn_in['Wu'], 'L1_attn_bu': _L1_attn_in['bu'], 'L1_ffn_wg1': _L1_ffn_in['wg1'], 'L1_ffn_bg1': _L1_ffn_in['bg1'], 'L1_ffn_wg2': _L1_ffn_in['wg2'], 'L1_ffn_w_in': _L1_ffn_in['w_in'], 'L1_ffn_w_out': _L1_ffn_in['w_out']}
    _x0 = _d['L0_attn_x']
    _d['L0_attn_x'] = jax.random.normal(jax.random.fold_in(jax.random.key(seed), 1), (4, 1024, 128), dtype=_x0.dtype)
    del _x0
    return _d

def reference(L0_attn_x, L0_attn_W_qkv, L0_attn_W_out, L0_ffn_w_freq_real, L0_ffn_w_freq_imag, L0_ffn_bias, L1_attn_Wq, L1_attn_Wk, L1_attn_Wv, L1_attn_Wu, L1_attn_bu, L1_ffn_wg1, L1_ffn_bg1, L1_ffn_wg2, L1_ffn_w_in, L1_ffn_w_out):

    def _L0_attn_ref(x, W_qkv, W_out):
        import jax, jax.numpy as jnp
        import numpy as np
        D_MODEL = 128
        N_HEADS = 16
        D_HEAD = D_MODEL // N_HEADS
        B, T, C = x.shape
        qkv = jnp.einsum('btc,oc->bto', x, W_qkv)
        q, k, v = jnp.split(qkv, 3, axis=-1)

        def split_heads(t):
            return t.reshape(B, T, N_HEADS, D_HEAD).transpose(0, 2, 1, 3)
        q, k, v = (split_heads(q), split_heads(k), split_heads(v))
        scale = D_HEAD ** (-0.5)
        scores = jnp.einsum('bhqd,bhkd->bhqk', q, k) * scale
        mask = jnp.triu(jnp.ones((T, T), dtype=bool), k=1)
        scores = jnp.where(mask, -jnp.inf, scores)
        att = jax.nn.softmax(scores, axis=-1)
        out = jnp.einsum('bhqk,bhkd->bhqd', att, v)
        out = out.transpose(0, 2, 1, 3).reshape(B, T, C)
        return jnp.einsum('btc,oc->bto', out, W_out)

    def _L0_ffn_ref(x, w_freq_real, w_freq_imag, bias):
        import jax, jax.numpy as jnp
        import numpy as np
        B, N, D = (4, 256, 128)
        SPARSITY = 0.01
        w = jax.lax.complex(w_freq_real, w_freq_imag)
        x_freq = jnp.fft.fft(x, axis=-1)
        y_freq = jnp.einsum('bnd,do->bno', x_freq, w)
        y = jnp.real(jnp.fft.ifft(y_freq, axis=-1))
        return y + bias

    def _L1_attn_ref(x, Wq, Wk, Wv, Wu, bu):
        import jax, jax.numpy as jnp
        import numpy as np
        B, T, EMB, HEADS = (4, 256, 128, 16)
        CHUNK = EMB // HEADS
        b, t, d = x.shape
        h = HEADS
        c = d // h
        xh = x.reshape(b, t, h, c)
        scale = d ** (-0.25)
        q = jnp.einsum('bthc,oc->btho', xh, Wq) * scale
        k = jnp.einsum('bthc,oc->btho', xh, Wk) * scale
        v = jnp.einsum('bthc,oc->btho', xh, Wv)
        scores = jnp.einsum('bihc,bjhc->bhij', q, k)
        i = jnp.arange(t)[:, None]
        j = jnp.arange(t)[None, :]
        scores = jnp.where(j > i, -jnp.inf, scores)
        attn = jax.nn.softmax(scores, axis=-1)
        y = jnp.einsum('bhij,bjhc->bihc', attn, v).reshape(b, t, d)
        return y @ Wu.T + bu

    def _L1_ffn_ref(x, wg1, bg1, wg2, w_in, w_out):
        import jax, jax.numpy as jnp
        import numpy as np
        B, S, D = (2, 128, 128)
        E, H, K, G = (8, 256, 2, 32)
        b, s, d = x.shape
        xt = x.reshape(-1, d)
        n = xt.shape[0]
        g = jax.nn.gelu(xt @ wg1 + bg1, approximate=False)
        logits = g @ wg2
        probs = jax.nn.softmax(logits, axis=-1)
        top_vals, top_idx = jax.lax.top_k(probs, K)
        gates = jnp.zeros_like(probs).at[jnp.arange(n)[:, None], top_idx].set(top_vals)
        h = jax.nn.gelu(jnp.einsum('nd,edh->enh', xt, w_in), approximate=False)
        o = jnp.einsum('enh,ehd->end', h, w_out)
        y = jnp.einsum('ne,end->nd', gates, o)
        return y.reshape(b, s, d)
    x = L0_attn_x
    x = x + _L0_attn_ref(_layernorm(x, axis=-1), L0_attn_W_qkv, L0_attn_W_out)
    x = x + _L0_ffn_ref(_layernorm(x, axis=-1), L0_ffn_w_freq_real, L0_ffn_w_freq_imag, L0_ffn_bias)
    x = x + _L1_attn_ref(_layernorm(x, axis=-1), L1_attn_Wq, L1_attn_Wk, L1_attn_Wv, L1_attn_Wu, L1_attn_bu)
    x = x + _L1_ffn_ref(_layernorm(x, axis=-1), L1_ffn_wg1, L1_ffn_bg1, L1_ffn_wg2, L1_ffn_w_in, L1_ffn_w_out)
    return x

_drawn_inputs = setup_inputs


def setup_inputs(seed=0):
    import zlib

    import numpy as np

    out = dict(_drawn_inputs(seed))
    spreads = {'L1_attn_bu': (0.0, 0.1), 'L1_ffn_bg1': (0.0, 0.8)}
    factors = {'L0_ffn_bias': 4.513,
     'L1_ffn_wg1': 8.0,
     'L1_ffn_wg2': 8.0,
     'L1_ffn_w_in': 8.0,
     'L1_ffn_w_out': 8.0}
    for name, (base, spread) in spreads.items():
        noise = np.random.default_rng([zlib.crc32(name.encode()), seed]).standard_normal(out[name].shape)
        drawn = base * np.exp(spread * noise) if base else spread * noise
        out[name] = jnp.asarray(drawn.astype(out[name].dtype))
    for name, factor in factors.items():
        out[name] = (out[name] * factor).astype(out[name].dtype)
    return out
```

```python
import numpy as np
import concourse.bass as bass
from concourse import mybir
from contextlib import ExitStack

FP32 = mybir.dt.float32
BF16 = mybir.dt.bfloat16
ALU = mybir.AluOpType
ACT = mybir.ActivationFunctionType
AX = mybir.AxisListType

B, T, D = 4, 1024, 128
HEADS = 16
DH = D // HEADS
P = 128
TT = T // P
NT = B * TT
E, HID, G = 8, 256, 32
HJ = HID // P
EPS = 1e-5
SCALE = (DH ** -0.5, D ** -0.5)

GH = 4
GROUPS = HEADS // GH
Q_PART = (0, 1, 2, 0, 1, 0)
K_PART = (0, 0, 0, 1, 1, 2)
SPLIT = DH * len(Q_PART)
SHIFT = 2
ROWS = SPLIT + SHIFT
LOW = -1.0e30

C_ID, C_COS, C_SIN, C_NSIN, C_TRI, C_HEAD, C_TIE, C_KEEP, C_END = np.cumsum([0, P, P, P, P, 512, HEADS, 64, P])

BANK = 512
SCORE_BANKS = 4
OUT_BANK = 4
RING_BANK = 6
NEXT = 8

SCORE_FILLS = [(hh, i, piece) for hh in range(GH) for i in range(TT)
               for piece in (("full", "diag") if i >= 4 else ("diag",))]
NF = len(SCORE_FILLS)
RING_PER_GROUP = NF + 1 + 2


def units_of_step(s):
    if s == 0:
        return [[(hh, 0, 0)] for hh in range(GH)]
    if s < 4:
        return [[(hh, s, 0), (hh, TT - s, T - P * s)] for hh in range(GH)]
    return [[(hh, 4, 0), (hh + 1, 4, 512)] for hh in (0, 2)]


STEPS = 5
UNITS = [len(units_of_step(s)) for s in range(STEPS)]
UNITS_PER_GROUP = sum(UNITS)


def unit_number(g, s, u):
    return g * UNITS_PER_GROUP + sum(UNITS[:s]) + u


def prob_slot(g, s, u):
    return 4 * ((g * STEPS + s) % 2) + u


def value_pieces(s):
    out = []
    for kb in {0: [0], 4: [4]}.get(s, [s, TT - s]):
        for half in (0, 1):
            q0, q1 = max(kb * P, half * BANK), (half + 1) * BANK
            if q0 < q1:
                out.append((kb, q0, q1 - q0, half))
    return out


def ring_of_groups(b_last):
    out = []
    for g in range(GROUPS):
        here = g + 1 if not (b_last and g + 1 >= GROUPS) else None
        after = g + 2 if not (b_last and g + 2 >= GROUPS) else None
        if here is not None:
            rest = [("score", here) + f for f in SCORE_FILLS[NEXT:]]
        else:
            rest = []
        if g > 0:
            rest[14:14] = [("out", g - 1, 0), ("out", g - 1, 1)]
        if after is not None:
            ahead = [("score", after) + f for f in SCORE_FILLS[:NEXT]]
            ahead[3:3] = [("shift", here)]
        else:
            ahead = [("shift", here)] if here is not None else []
        out.append(rest + ahead)
    return out


def first_ring():
    ahead = [("score", 1) + f for f in SCORE_FILLS[:NEXT]]
    ahead[3:3] = [("shift", 0)]
    return [("score", 0) + f for f in SCORE_FILLS] + ahead


def batch_order(last):
    rings = ring_of_groups(last)
    order, pending = [], []
    for g in range(GROUPS):
        main = []
        for s in range(STEPS):
            here = [("unit", g, s, u) for u in range(UNITS[s])]
            n = max(1, len(here) // 2)
            mixed = here[:n]
            rest = here[n:]
            for j, v in enumerate(pending):
                mixed.append(v)
                if rest:
                    mixed.append(rest.pop(0))
            main += mixed + rest
            pending = [("values", g, s, n) for n in range(len(value_pieces(s)))]
        ring = rings[g]
        total = len(main)
        done = 0
        for n, m in enumerate(main):
            order.append(m)
            while (done + 1) * total <= len(ring) * (n + 1):
                order.append(ring[done])
                done += 1
        order += ring[done:]
    order += pending
    order += [("out", GROUPS - 1, 0), ("out", GROUPS - 1, 1)]
    return order


ORDER = {last: batch_order(last) for last in (False, True)}
RING = {last: [x for x in ORDER[last] if x[0] in ("score", "shift", "out")] for last in (False, True)}
FIRST = first_ring()
RING_FIRST = len(FIRST)
RING_BATCH = len(RING[False])


class Memory:

    def __init__(self, nc, ctx):
        def sb(name, shape, dt=FP32):
            return ctx.enter_context(nc.sbuf_tensor(name, shape, dt))

        self.x = sb("x", [P, NT, D])
        self.const = sb("const", [P, int(C_END)])
        self.ident_bf = sb("ident_bf", [P, P], BF16)
        self.raw = sb("raw", [P, 8, P])
        self.w = sb("w", [P, 9, P])
        self.w8 = sb("w8", [DH, 3, DH])
        self.w8r = sb("w8r", [DH, 3, HEADS, DH])
        self.dft = sb("dft", [P, 2, P])
        self.bias_ffn = sb("bias_ffn", [P, D])
        self.bias_u = sb("bias_u", [P, D])
        self.v = sb("v", [P, NT, D])
        self.att = sb("att", [P, NT, D])
        self.att_b = sb("att_b", [P, TT, D])
        self.xn = sb("xn", [P, TT, D])
        self.xn_t = sb("xn_t", [P, T])
        self.att_t = sb("att_t", [P, T])
        self.stats = sb("stats", [P, TT, 6])
        self.mv = sb("mv", [P, TT, 2])
        self.std = sb("std", [P, TT])
        self.rstd = sb("rstd", [P, TT])
        self.eps = sb("eps", [P, 1])
        self.q_rows = sb("q_rows", [P, GROUPS, 2, T], BF16)
        self.k_rows = sb("k_rows", [P, GROUPS, 2, T], BF16)
        self.probs = sb("probs", [P, 8, T])
        self.vg = sb("vg", [P, 2, TT, GH, 32])
        self.out_t = sb("out_t", [P, T])
        self.max_a = sb("max_a", [P, 2, 2, 2, TT])
        self.max_b = sb("max_b", [P, 2, 2, 2, TT])
        self.shift = sb("shift", [P, 2, SHIFT, 2 * TT], BF16)
        self.shift_t = sb("shift_t", [2 * SHIFT * 2 * TT, P], BF16)
        self.scrap = sb("scrap", [P, 2, BANK], BF16)
        self.rden = sb("rden", [P, 2, 4 * GH])
        self.w_in = sb("w_in", [P, E, HID])
        self.w_out = sb("w_out", [P, E, HJ, D])
        self.wg1 = sb("wg1", [P, G])
        self.bg1 = sb("bg1", [G, 1])
        self.wg2 = sb("wg2", [G, E])
        self.gate = sb("gate", [P, 5, TT * E])
        self.gate_pairs = sb("gate_pairs", [P, 2, TT * E, E])
        self.gate_col = sb("gate_col", [P, 3, TT])
        self.psum = ctx.enter_context(nc.psum_tensor("psum", [P, 8, BANK], FP32))
        self.q_dram = nc.dram_tensor("q_split", (HEADS, SPLIT, B * T), BF16, kind="Internal").ap()
        self.k_dram = nc.dram_tensor("k_split", (HEADS, SPLIT, B * T), BF16, kind="Internal").ap()

    def split(self, n):
        return self.probs[:, 5 + n // 2, :].bitcast(BF16)[:, (n % 2) * T:(n % 2 + 1) * T]


Q0, K0, V0, O0, Q1, K1, V1, O1, CIRC = range(9)


def stand(engine, semaphore, value, passed):
    engine.wait_ge(semaphore, value)
    engine.sem_inc(passed, 1)


def setup(nc, m, dram, sem):
    ident = m.const[:, C_ID:C_COS]
    cos, sin, nsin = (m.const[:, c:c + P] for c in (C_COS, C_SIN, C_NSIN))
    loaded, head_loaded, repeated, made, used, half, ready = (
        sem(n) for n in ("setup_loaded", "setup_w8_loaded", "setup_w8_repeated", "setup_psum", "setup_evacuated",
                         "setup_half", "setup_ready"))
    x_loaded, bias_loaded, own = sem("setup_x_loaded"), sem("setup_bias_loaded"), sem("setup_memset")
    with nc.Block() as block:
        @block.sync
        def _(sp):
            sp.dma_start(m.const[:, :], dram["consts"]).then_inc(loaded, 16)
            sp.dma_start(m.raw[:, 0:3, :], dram["L0_attn_W_qkv"].rearrange("(n o) c -> o n c", o=P)).then_inc(loaded, 16)
            sp.dma_start(m.raw[:, 3, :], dram["L0_attn_W_out"]).then_inc(loaded, 16)
            sp.dma_start(m.raw[:, 4, :], dram["L1_attn_Wu"]).then_inc(loaded, 16)
            sp.dma_start(m.raw[:, 5, :], dram["L0_ffn_w_freq_real"]).then_inc(loaded, 16)
            sp.dma_start(m.raw[:, 6, :], dram["L0_ffn_w_freq_imag"]).then_inc(loaded, 16)
            sp.dma_start(m.x[:, :, :], dram["L0_attn_x"].rearrange("b (t p) d -> p (b t) d", p=P)).then_inc(x_loaded, 16)
            sp.dma_start(m.w_in[:, :, :], dram["L1_ffn_w_in"].rearrange("e d h -> d e h")).then_inc(x_loaded, 16)
            sp.dma_start(m.w_out[:, :, :, :], dram["L1_ffn_w_out"].rearrange("e (j h) d -> h e j d", h=P)).then_inc(x_loaded, 16)
            sp.wait_ge(x_loaded, 3 * 16)

        @block.scalar
        def _(act):
            for n, name in enumerate(("L1_attn_Wq", "L1_attn_Wk", "L1_attn_Wv")):
                act.dma_start(m.w8[:, n, :], dram[name]).then_inc(head_loaded, 16)
            act.dma_start(m.bias_ffn[:, :], dram["L0_ffn_bias"].rearrange("(a d) -> a d", a=1).broadcast_to([P, D])).then_inc(bias_loaded, 16)
            act.dma_start(m.bias_u[:, :], dram["L1_attn_bu"].rearrange("(a d) -> a d", a=1).broadcast_to([P, D])).then_inc(bias_loaded, 16)
            act.dma_start(m.wg1[:, :], dram["L1_ffn_wg1"]).then_inc(bias_loaded, 16)
            act.dma_start(m.bg1[:, :], dram["L1_ffn_bg1"].rearrange("(g a) -> g a", a=1)).then_inc(bias_loaded, 16)
            act.dma_start(m.wg2[:, :], dram["L1_ffn_wg2"]).then_inc(bias_loaded, 16)
            act.wait_ge(bias_loaded, 5 * 16)

        @block.gpsimd
        def _(pool):
            nc.gpsimd.memset(m.eps[:, :], EPS).then_inc(own, 1)
            nc.gpsimd.memset(m.k_rows[:, :, :, :], 1.0).then_inc(own, 1)
            nc.gpsimd.memset(m.vg[:, :, :, :, :], 0.0).then_inc(own, 1)
            pool.wait_ge(own, 3)
            nc.gpsimd.memset(m.vg[:, :, :, :, DH:DH + 1], 1.0).then_inc(own, 1)
            pool.wait_ge(own, 4)

        @block.vector
        def _(dve):
            dve.wait_ge(head_loaded, 3 * 16)
            for n in range(3):
                nc.vector.tensor_copy(m.w8r[:, n, :, :], m.w8[:, n, :].unsqueeze(1).broadcast_to([DH, HEADS, DH])).then_inc(repeated, 1)
            dve.wait_ge(loaded, 6 * 16)
            nc.vector.tensor_copy(m.ident_bf[:, :], ident).then_inc(ready, 1)
            dve.wait_ge(made, 1)
            nc.vector.tensor_copy(m.w[:, Q0:O0 + 1, :].rearrange("p a b -> p (a b)"), m.psum[:, 0, :]).then_inc(used, 1)
            dve.wait_ge(made, 2)
            for n in range(3):
                nc.vector.tensor_tensor(
                    m.w[:, Q1 + n, :].rearrange("p (h o) -> p h o", o=DH),
                    m.psum[:, 1, n * DH:(n + 1) * DH].unsqueeze(1).broadcast_to([P, HEADS, DH]),
                    m.const[:, C_HEAD:C_TIE].unsqueeze(2).broadcast_to([P, HEADS, DH]), ALU.mult).then_inc(used, 1)
            nc.vector.tensor_copy(m.w[:, O1, :], m.psum[:, 1, P:2 * P]).then_inc(used, 1)
            dve.wait_ge(made, 3)
            nc.vector.tensor_copy(m.dft[:, :, :].rearrange("p a b -> p (a b)"), m.psum[:, 2, 0:2 * P]).then_inc(half, 1)
            dve.wait_ge(made, 4)
            nc.vector.tensor_scalar(m.w[:, CIRC, :], m.psum[:, 3, 0:P], 1.0 / D, None, ALU.mult).then_inc(used, 1)
            dve.wait_ge(used, 6)
            dve.wait_ge(ready, 1)

        @block.tensor
        def _(pe):
            pe.wait_ge(loaded, 6 * 16)
            for n in range(4):
                last = nc.tensor.transpose(m.psum[:, 0, n * P:(n + 1) * P], m.raw[:, n, :], ident)
            last.then_inc(made, 1)
            pe.wait_ge(repeated, 3)
            for n in range(3):
                nc.tensor.matmul(m.psum[:, 1, n * DH:(n + 1) * DH], m.w8r[:, n, :, :].rearrange("o h c -> o (h c)"),
                                 ident[0:DH, 0:DH], start=True, stop=True)
            nc.tensor.transpose(m.psum[:, 1, P:2 * P], m.raw[:, 4, :], ident).then_inc(made, 1)
            real, imag = m.raw[:, 5, :], m.raw[:, 6, :]
            nc.tensor.matmul(m.psum[:, 2, 0:P], real, cos, start=True, stop=False)
            nc.tensor.matmul(m.psum[:, 2, 0:P], imag, sin, start=False, stop=True)
            nc.tensor.matmul(m.psum[:, 2, P:2 * P], imag, cos, start=True, stop=False)
            nc.tensor.matmul(m.psum[:, 2, P:2 * P], real, nsin, start=False, stop=True).then_inc(made, 1)
            pe.wait_ge(half, 1)
            nc.tensor.matmul(m.psum[:, 3, 0:P], m.dft[:, 0, :], cos, start=True, stop=False)
            nc.tensor.matmul(m.psum[:, 3, 0:P], m.dft[:, 1, :], nsin, start=False, stop=True).then_inc(made, 1)


def deviations(nc, m, act, b, step, std_ready):
    act.wait_ge(step, NORM_STEPS * b + 2 * TT)
    nc.scalar.activation(m.std[:, :], m.mv[:, :, 1], ACT.Sqrt, bias=m.eps[:, :]).then_inc(std_ready, 1)


def normalise(nc, m, dve, b, step, std_ready, xn_ready):
    x = m.x[:, :, :].rearrange("p (b t) d -> p b t d", b=B)
    dve.sem_inc(m.passed, 1)
    for t in range(TT):
        nc.vector.bn_stats(m.stats[:, t, :], x[:, b, t, :]).then_inc(step, 1)
    stand(dve, step, NORM_STEPS * b + TT, m.passed)
    for t in range(TT):
        nc.vector.bn_aggr(m.mv[:, t, :], m.stats[:, t, :]).then_inc(step, 1)
    dve.wait_ge(std_ready, b + 1)
    nc.vector.reciprocal(m.rstd[:, :], m.std[:, :]).then_inc(step, 1)
    dve.wait_ge(step, NORM_STEPS * b + 2 * TT + 1)
    for t in range(TT):
        last = nc.vector.tensor_scalar(m.xn[:, t, :], x[:, b, t, :], m.mv[:, t, 0:1], m.rstd[:, t:t + 1],
                                       ALU.subtract, ALU.mult)
        if t % 4 == 3:
            last.then_inc(xn_ready, 1)


NORM_STEPS = 2 * TT + 1


def transposes(nc, m, pe, src, bank, turned):
    for half in (0, 1):
        for t in range(4):
            last = nc.tensor.transpose(m.psum[:, bank + half, t * P:(t + 1) * P], src(4 * half + t), m.const[:, C_ID:C_COS])
        last.then_inc(turned, 1)


def project_tokens(nc, m, src_t, weight, bank, made):
    for t in range(TT):
        last = nc.tensor.matmul(m.psum[:, bank + t // 4, (t % 4) * P:(t % 4 + 1) * P], src_t[:, t * P:(t + 1) * P],
                                weight, start=True, stop=True)
    last.then_inc(made, 1)


def prepare(nc, m, layer, sem):
    wq, wk, wv = ((Q0, K0, V0), (Q1, K1, V1))[layer]
    names = ("ln_step", "std_ready", "xn_ready", "turned", "xnt_ready", "q_made", "k_made", "v_made", "high_made", "rest_made",
             "middle_made", "low_made", "v_copied", "stored")
    (ln_step, std_ready, xn_ready, turned, xnt_ready, q_made, k_made, v_made, high_made, rest_made, middle_made, low_made,
     v_copied, stored) = (sem(f"prep{layer}_{n}") for n in names)
    STORES = 2 * len(Q_PART) * 16
    scales = (SCALE[layer], 1.0)
    QB, KB, VB = 2, 4, 6
    with nc.Block() as block:
        @block.vector
        def _(dve):
            with dve.Fori(0, B) as b:
                dve.wait_ge(turned, 2 * b)
                normalise(nc, m, dve, b, ln_step, std_ready, xn_ready)
                dve.wait_ge(stored, STORES * b)
                for n, bank in ((0, QB), (1, KB)):
                    dve.wait_ge(high_made, 2 * b + n + 1)
                    nc.vector.scalar_tensor_tensor(m.probs[:, 3 + n, :], m.psum[:, bank:bank + 2, :].rearrange("p a b -> p (a b)"),
                                                   scales[n], m.split(3 * n), ALU.mult, ALU.subtract).then_inc(rest_made, 1)
                for n in (0, 1):
                    dve.wait_ge(rest_made, 2 * b + n + 1)
                    nc.vector.tensor_copy(m.split(3 * n + 1), m.probs[:, 3 + n, :]).then_inc(middle_made, 1)
                for n in (0, 1):
                    dve.wait_ge(middle_made, 2 * b + n + 1)
                    nc.vector.tensor_tensor(m.split(3 * n + 2), m.probs[:, 3 + n, :], m.split(3 * n + 1),
                                            ALU.subtract).then_inc(low_made, 1)

        @block.scalar
        def _(act):
            v = m.v[:, :, :].rearrange("p (b t) d -> p b (t d)", b=B)
            with act.Fori(0, B) as b:
                deviations(nc, m, act, b, ln_step, std_ready)
                act.wait_ge(v_made, b)
                for half in (0, 1):
                    act.wait_ge(turned, 2 * b + half + 1)
                    nc.scalar.activation(m.xn_t[:, half * BANK:(half + 1) * BANK], m.psum[:, half, :], ACT.Copy).then_inc(xnt_ready, 1)
                act.wait_ge(stored, STORES * b)
                for n, bank, made in ((0, QB, q_made), (1, KB, k_made)):
                    act.wait_ge(made, b + 1)
                    nc.scalar.activation(m.split(3 * n), m.psum[:, bank:bank + 2, :].rearrange("p a b -> p (a b)"),
                                         ACT.Copy, scale=scales[n]).then_inc(high_made, 1)
                act.wait_ge(v_made, b + 1)
                nc.scalar.activation(v[:, b, :], m.psum[:, VB:VB + 2, :].rearrange("p a b -> p (a b)"), ACT.Copy).then_inc(v_copied, 1)

        @block.tensor
        def _(pe):
            with pe.Fori(0, B) as b:
                pe.wait_ge(xn_ready, 2 * b + 2)
                transposes(nc, m, pe, lambda t: m.xn[:, t, :], 0, turned)
                pe.wait_ge(xnt_ready, 2 * b + 2)
                pe.wait_ge(rest_made, 2 * b)
                pe.wait_ge(v_copied, b)
                for weight, bank, made in ((wq, QB, q_made), (wk, KB, k_made)):
                    for half in (0, 1):
                        last = nc.tensor.matmul(m.psum[:, bank + half, :], m.w[:, weight, :],
                                                m.xn_t[:, half * BANK:(half + 1) * BANK], start=True, stop=True)
                    last.then_inc(made, 1)
                project_tokens(nc, m, m.xn_t, m.w[:, wv, :], VB, v_made)

        @block.sync
        def _(sp):
            dests = [d.rearrange("h (r d) (b t) -> r b h d t", d=DH, b=B) for d in (m.q_dram, m.k_dram)]
            with sp.Fori(0, B) as b:
                sp.wait_ge(high_made, 2 * b + 2)
                sp.wait_ge(middle_made, 2 * b + 2)
                sp.wait_ge(low_made, 2 * b + 2)
                for n, parts in ((0, Q_PART), (1, K_PART)):
                    for r, part in enumerate(parts):
                        sp.dma_start(dests[n][r, b], m.split(3 * n + part)).then_inc(stored, 16)
            sp.wait_ge(stored, STORES * B)


def attention(nc, m, layer, sem):
    ring_filled, ring_read, shift_ready, shift_loaded = (
        sem(f"att{layer}_{n}") for n in ("ring_filled", "ring_read", "shift_ready", "shift_loaded"))
    rows_loaded = [sem(f"att{layer}_rows_loaded{n}") for n in range(GROUPS)]
    unit_filled, exp_done, masked, values_done, vg_ready, out_copied, den_ready, max_step = (
        sem(f"att{layer}_{n}") for n in ("unit_filled", "exp_done", "masked", "values_done", "vg_ready", "out_copied",
                                         "den_ready", "max_step"))
    UB = GROUPS * UNITS_PER_GROUP
    SB = GROUPS * STEPS
    LOADS = 4 * 16

    def ring_count(b, n):
        return n if b is None else RING_FIRST + RING_BATCH * b + n

    def ring_bank(b, n):
        return RING_BANK + (n if b is None else RING_FIRST + n) % 2

    def group_count(b, g):
        return g if b is None else GROUPS * b + g

    def over_batches(engine, body):
        with engine.Fori(0, B - 1) as b:
            body(b, False)
        body(B - 1, True)

    def head(g, hh):
        return 64 * (hh % 2), g % GROUPS, hh // 2

    with nc.Block() as block:
        @block.sync
        def _(sp):
            def load(g, b):
                for rows, d in ((m.q_rows, m.q_dram), (m.k_rows, m.k_dram)):
                    src = d.rearrange("(g j a) r (b t) -> a g b r j t", a=2, j=2, b=B)
                    for a in (0, 1):
                        sp.dma_start(rows[64 * a:64 * a + SPLIT, g % GROUPS, :, :], src[a, g % GROUPS, b]).then_inc(
                            rows_loaded[g % GROUPS], 16)

            def store_shift(g, copied):
                sp.wait_ge(ring_read, copied)
                for a in (0, 1):
                    dst = m.q_rows[64 * a + SPLIT:64 * a + ROWS, g % GROUPS, :, :].rearrange("s j (i t) -> s (j i) t", t=P)
                    sp.dma_start(dst, m.shift_t[32 * a:32 * a + 32, :]).then_inc(shift_loaded, 16)

            load(0, 0)
            load(1, 0)
            store_shift(0, FIRST.index(("shift", 0)) + 1)

            def body(b, last):
                for g in range(GROUPS):
                    if not (last and g + 2 >= GROUPS):
                        sp.wait_ge(unit_filled, UB * b + UNITS_PER_GROUP * g)
                        load(g + 2, b + (g + 2) // GROUPS)
                    if not (last and g + 1 >= GROUPS):
                        store_shift(g + 1, ring_count(b, RING[last].index(("shift", g + 1)) + 1))
            over_batches(sp, body)
            sp.wait_ge(shift_loaded, 32 * B * GROUPS)

        @block.tensor
        def _(pe):
            def fill_ring(item, b, n):
                kind, g = item[0], item[1]
                bank = ring_bank(b, n)
                if not (b is None and n < 2):
                    pe.wait_ge(ring_read, ring_count(b, n) - 1)
                if kind == "score":
                    hh, i, piece = item[2:]
                    row, buf, j = head(g, hh)
                    if (hh, i) == (0, 0):
                        pe.wait_ge(rows_loaded[g % GROUPS], LOADS * ((0 if b is None else b) + g // GROUPS + 1))
                    k0 = 0 if piece == "full" or i < 4 else BANK
                    width = BANK if piece == "full" else P * (i + 1) - k0
                    done = nc.tensor.matmul(m.psum[:, bank, 0:width], m.q_rows[row:row + SPLIT, buf, j, i * P:(i + 1) * P],
                                            m.k_rows[row:row + SPLIT, buf, j, k0:k0 + width], start=True, stop=True)
                elif kind == "shift":
                    stand(pe, shift_ready, group_count(b, g) + 1, m.passed)
                    done = nc.tensor.transpose(m.psum[0:64, bank, 0:P // 2].bitcast(BF16),
                                               m.shift[:, :, :, :].rearrange("p a s n -> p (a s n)"), m.ident_bf[:, :])
                else:
                    half = item[2]
                    pe.wait_ge(out_copied, GROUPS * b + g + 1)
                    for t in range(4):
                        done = nc.tensor.transpose(m.psum[:, bank, t * P:(t + 1) * P],
                                                   m.out_t[:, half * BANK + t * P:half * BANK + (t + 1) * P], m.const[:, C_ID:C_COS])
                done.then_inc(ring_filled, 1)

            for n, item in enumerate(FIRST):
                fill_ring(item, None, n)

            def body(b, last):
                n_ring = 0
                for item in ORDER[last]:
                    if item[0] == "unit":
                        g, s, u = item[1:]
                        n = unit_number(g, s, u)
                        slot = n % 2
                        if (s, u) == (0, 0):
                            pe.wait_ge(shift_loaded, 32 * (GROUPS * b + g + 1))
                        if isinstance(b, int) or n >= 1:
                            pe.wait_ge(exp_done, UB * b + n - 1)
                        else:
                            pe.wait_ge(exp_done, UB * b)
                        for hh, kb, col in units_of_step(s)[u]:
                            row, buf, j = head(g, hh)
                            width = min(T - P * kb, T - col, BANK if s == 4 else T)
                            c = col
                            while c < col + width:
                                w = min(col + width, (c // BANK + 1) * BANK) - c
                                q0 = kb * P + c - col
                                done = nc.tensor.matmul(
                                    m.psum[:, 2 * slot + c // BANK, c % BANK:c % BANK + w],
                                    m.k_rows[row:row + ROWS, buf, j, kb * P:(kb + 1) * P],
                                    m.q_rows[row:row + ROWS, buf, j, q0:q0 + w], start=True, stop=True)
                                c += w
                        done.then_inc(unit_filled, 1)
                    elif item[0] == "values":
                        g, s, n = item[1:]
                        kb, q0, w, half = value_pieces(s)[n]
                        if n == 0:
                            pe.wait_ge(masked, UB * b + unit_number(g, s, UNITS[s] - 1) + 1)
                            if s == 0:
                                pe.wait_ge(vg_ready, GROUPS * b + g + 1)
                                pe.wait_ge(out_copied, GROUPS * b + g)
                        for hh in range(GH):
                            u, col = [(u, c) for u, unit in enumerate(units_of_step(s)) for h2, k2, c in unit
                                      if (h2, k2) == (hh, kb)][0]
                            c = col + q0 - kb * P
                            done = nc.tensor.matmul(
                                m.psum[32 * hh:32 * hh + 32, OUT_BANK + half, q0 % BANK:q0 % BANK + w],
                                m.vg[:, g % 2, kb, hh, :], m.probs[:, prob_slot(g, s, u), c:c + w],
                                start=(kb == 0), stop=(kb == (3, 4)[half]), tile_position=(0, 32 * hh))
                        if n == len(value_pieces(s)) - 1:
                            done.then_inc(values_done, 1)
                    else:
                        fill_ring(item, b, n_ring)
                        n_ring += 1
            over_batches(pe, body)

        @block.scalar
        def _(act):
            def body(b, last):
                def copy_out(g):
                    act.wait_ge(values_done, SB * b + STEPS * (g + 1))
                    if g > 0:
                        act.wait_ge(ring_filled, ring_count(b, RING[last].index(("out", g - 1, 1)) + 1))
                    nc.scalar.activation(m.out_t[:, :], m.psum[:, OUT_BANK:OUT_BANK + 2, :].rearrange("p a b -> p (a b)"),
                                         ACT.Copy).then_inc(out_copied, 1)

                for g in range(GROUPS):
                    for s in range(STEPS):
                        for u in range(UNITS[s]):
                            n = unit_number(g, s, u)
                            act.wait_ge(unit_filled, UB * b + n + 1)
                            if u == 0:
                                if isinstance(b, int) or g * STEPS + s >= 2:
                                    act.wait_ge(values_done, SB * b + g * STEPS + s - 1)
                                else:
                                    act.wait_ge(values_done, SB * b)
                            nc.scalar.activation(m.probs[:, prob_slot(g, s, u), :],
                                                 m.psum[:, 2 * (n % 2):2 * (n % 2) + 2, :].rearrange("p a b -> p (a b)"),
                                                 ACT.Exp).then_inc(exp_done, 1)
                            if (s, u) == (0, 2) and g > 0:
                                copy_out(g - 1)
                copy_out(GROUPS - 1)
            over_batches(act, body)

        @block.gpsimd
        def _(pool):
            v = m.v[:, :, :].rearrange("p (b t) (g h d) -> p b g t h d", b=B, g=GROUPS, h=GH)

            def lay_values(g, b):
                nc.gpsimd.tensor_copy(m.vg[:, g % 2, :, :, 0:DH], v[:, b + g // GROUPS, g % GROUPS]).then_inc(vg_ready, 1)

            lay_values(0, 0)

            def body(b, last):
                for g in range(GROUPS):
                    for s in range(STEPS):
                        for u, unit in enumerate(units_of_step(s)):
                            pool.wait_ge(exp_done, UB * b + unit_number(g, s, u) + 1)
                            for _, _, col in unit:
                                block_ = m.probs[:, prob_slot(g, s, u), col:col + P]
                                done = nc.gpsimd.tensor_tensor(block_, block_, m.const[:, C_KEEP:C_END], ALU.mult)
                            done.then_inc(masked, 1)
                        if s == 2 and not (last and g + 1 >= GROUPS):
                            pool.wait_ge(values_done, SB * b + STEPS * g)
                            lay_values(g + 1, b)
            over_batches(pool, body)

        @block.vector
        def _(dve):
            def take(item, b, n):
                kind, g = item[0], item[1]
                bank = ring_bank(b, n)
                if kind == "score" and item[4] == "diag" and b is not None:
                    stand(dve, ring_filled, ring_count(b, n) + 1, m.passed)
                else:
                    dve.wait_ge(ring_filled, ring_count(b, n) + 1)
                if kind == "score":
                    hh, i, piece = item[2:]
                    a, j = hh % 2, hh // 2
                    if piece == "full":
                        nc.vector.tensor_reduce(m.max_b[:, g % 2, a, j, i:i + 1], m.psum[:, bank, :], axis=AX.X, op=ALU.max).then_inc(ring_read, 1)
                    else:
                        width = P * (i % 4 + 1)
                        nc.vector.tensor_tensor_reduce(
                            out=m.scrap[:, bank - RING_BANK, 0:width], in0=m.psum[:, bank, 0:width],
                            in1=m.const[:, C_TRI + BANK - width:C_TRI + BANK], scale=1.0, scalar=-3.0e38,
                            op0=ALU.add, op1=ALU.max, accum_out=m.max_a[:, g % 2, a, j, i:i + 1]).then_inc(ring_read, 1)
                    if (hh, i, piece) == SCORE_FILLS[-1]:
                        dve.wait_ge(ring_read, ring_count(b, n) + 1)
                        late = m.max_a[:, g % 2, :, :, 4:TT]
                        nc.vector.tensor_tensor(late, late, m.max_b[:, g % 2, :, :, 4:TT], ALU.max).then_inc(max_step, 1)
                        dve.wait_ge(max_step, 2 * group_count(b, g) + 1)
                        flat = m.max_a[:, g % 2, :, :, :].rearrange("p a j i -> p a (j i)")
                        nc.vector.tensor_scalar(m.shift[:, :, 0, :], flat, -1.0, None, ALU.mult).then_inc(max_step, 1)
                        dve.wait_ge(max_step, 2 * group_count(b, g) + 2)
                        nc.vector.scalar_tensor_tensor(m.shift[:, :, 1, :], flat, -1.0, m.shift[:, :, 0, :],
                                                       ALU.mult, ALU.subtract).then_inc(shift_ready, 1)
                elif kind == "shift":
                    if b is not None:
                        dve.wait_ge(shift_loaded, 32 * group_count(b, g))
                    nc.vector.tensor_copy(m.shift_t[:, :], m.psum[0:64, bank, 0:P // 2].bitcast(BF16)).then_inc(ring_read, 1)
                else:
                    half = item[2]
                    att = m.att[:, :, :].rearrange("p (b f t) (g h d) -> p b f g t h d", b=B, f=2, g=GROUPS, h=GH)[:, b, half, g]
                    outs = m.psum[:, bank, :].rearrange("p (t h c) -> p t h c", t=4, h=GH)
                    rden = m.rden[:, half, :].rearrange("p (t h) -> p t h", t=4)
                    nc.vector.reciprocal(rden, outs[:, :, :, DH]).then_inc(den_ready, 1)
                    dve.wait_ge(den_ready, 2 * (GROUPS * b + g) + half + 1)
                    nc.vector.tensor_tensor(att, outs[:, :, :, 0:DH], rden.unsqueeze(3).broadcast_to([P, 4, GH, DH]),
                                            ALU.mult).then_inc(ring_read, 1)

            for n, item in enumerate(FIRST):
                take(item, None, n)

            def body(b, last):
                for n, item in enumerate(RING[last]):
                    take(item, b, n)
            over_batches(dve, body)


def finish(nc, m, layer, out, sem):
    names = ("att_turned", "att_t_ready", "att_made", "att_added", "ln_step", "std_ready", "xn_ready", "xn_turned", "xnt_ready",
             "ffn_made", "ffn_added", "gate_hidden", "gate_gelu", "logits_made", "gate_step", "logits_moved",
             "gate_exp", "gate_ready", "att_moved", "hidden_made", "gelu_done", "expert_made", "mixed", "stored")
    (att_turned, att_t_ready, att_made, att_added, ln_step, std_ready, xn_ready, xn_turned, xnt_ready, ffn_made, ffn_added,
     gate_hidden, gate_gelu, logits_made, gate_step, logits_moved, gate_exp, gate_ready, att_moved, hidden_made, gelu_done,
     expert_made, mixed, stored) = (sem(f"fin{layer}_{n}") for n in names)
    wo = (O0, O1)[layer]
    moe = layer == 1
    ATT_T, MADE, XN_T, FFN = 0, 4, 2, 6
    GELUS = E * HJ
    GATE_STEPS = 9
    gate = m.gate
    gate_g = m.probs[0:G, 4, :]

    def flat(ap):
        return ap.rearrange("p a b -> p (a b)")

    with nc.Block() as block:
        @block.tensor
        def _(pe):
            with pe.Fori(0, B) as b:
                if moe:
                    pe.wait_ge(gelu_done, GELUS * b)
                    pe.wait_ge(mixed, E * b)
                pe.wait_ge(att_moved, b + 1)
                transposes(nc, m, pe, lambda t: m.att_b[:, t, :], ATT_T, att_turned)
                pe.wait_ge(att_t_ready, 2 * b + 2)
                project_tokens(nc, m, m.att_t, m.w[:, wo, :], MADE, att_made)
                pe.wait_ge(xn_ready, 2 * b + 2)
                transposes(nc, m, pe, lambda t: m.xn[:, t, :], XN_T, xn_turned)
                pe.wait_ge(xnt_ready, 2 * b + 2)
                if not moe:
                    pe.wait_ge(ffn_added, 3 * b)
                    project_tokens(nc, m, m.xn_t, m.w[:, CIRC, :], FFN, ffn_made)
                else:
                    for half in (0, 1):
                        last = nc.tensor.matmul(m.psum[0:G, FFN + half, :], m.wg1[:, :], m.xn_t[:, half * BANK:(half + 1) * BANK],
                                                start=True, stop=True)
                    last.then_inc(gate_hidden, 1)
                    pe.wait_ge(gate_gelu, b + 1)
                    for t in range(TT):
                        last = nc.tensor.matmul(m.psum[:, MADE, t * E:(t + 1) * E], gate_g[:, t * P:(t + 1) * P], m.wg2[:, :],
                                                start=True, stop=True)
                    last.then_inc(logits_made, 1)

                    def hidden(e):
                        for j in range(HJ):
                            if e > 0:
                                pe.wait_ge(gelu_done, GELUS * b + HJ * (e - 1) + j + 1)
                            for half in (0, 1):
                                last = nc.tensor.matmul(m.psum[:, 2 * j + half, :], m.w_in[:, e, j * P:(j + 1) * P],
                                                        m.xn_t[:, half * BANK:(half + 1) * BANK], start=True, stop=True)
                            last.then_inc(hidden_made, 1)

                    def expert(e):
                        bank = 4 + 2 * (e % 2)
                        pe.wait_ge(gelu_done, GELUS * b + HJ * (e + 1))
                        if e == 0:
                            pe.wait_ge(logits_moved, b + 1)
                        elif e >= 2:
                            pe.wait_ge(mixed, E * b + e - 1)
                        for t in range(TT):
                            for j in range(HJ):
                                last = nc.tensor.matmul(m.psum[:, bank + t // 4, (t % 4) * P:(t % 4 + 1) * P],
                                                        m.probs[:, 2 * (e % 2) + j, t * P:(t + 1) * P], m.w_out[:, e, j, :],
                                                        start=(j == 0), stop=(j == HJ - 1))
                        last.then_inc(expert_made, 1)

                    hidden(0)
                    for e in range(E):
                        if e + 1 < E:
                            hidden(e + 1)
                        expert(e)

        @block.scalar
        def _(act):
            with act.Fori(0, B) as b:
                act.wait_ge(att_made, b)
                for half in (0, 1):
                    act.wait_ge(att_turned, 2 * b + half + 1)
                    nc.scalar.activation(m.att_t[:, half * BANK:(half + 1) * BANK], m.psum[:, ATT_T + half, :], ACT.Copy).then_inc(att_t_ready, 1)
                deviations(nc, m, act, b, ln_step, std_ready)
                if moe:
                    act.wait_ge(expert_made, E * b)
                else:
                    act.wait_ge(ffn_made, b)
                for half in (0, 1):
                    act.wait_ge(xn_turned, 2 * b + half + 1)
                    nc.scalar.activation(m.xn_t[:, half * BANK:(half + 1) * BANK], m.psum[:, XN_T + half, :], ACT.Copy).then_inc(xnt_ready, 1)
                if moe:
                    act.wait_ge(gate_hidden, b + 1)
                    nc.scalar.activation(gate_g, flat(m.psum[0:G, FFN:FFN + 2, :]), ACT.Gelu, bias=m.bg1[:, :]).then_inc(gate_gelu, 1)
                    act.wait_ge(logits_moved, b + 1)
                    nc.scalar.activation(gate[:, 1, :], gate[:, 0, :], ACT.Exp).then_inc(gate_exp, 1)
                    for e in range(E):
                        if e >= 2:
                            act.wait_ge(expert_made, E * b + e - 1)
                        for j in range(HJ):
                            act.wait_ge(hidden_made, GELUS * b + HJ * e + j + 1)
                            nc.scalar.activation(m.probs[:, 2 * (e % 2) + j, :], flat(m.psum[:, 2 * j:2 * j + 2, :]), ACT.Gelu).then_inc(gelu_done, 1)

        @block.gpsimd
        def _(pool):
            att = m.att[:, :, :].rearrange("p (b t) d -> p b (t d)", b=B)
            with pool.Fori(0, B) as b:
                pool.wait_ge(att_turned, 2 * b)
                nc.gpsimd.tensor_copy(flat(m.att_b[:, :, :]), att[:, b, :]).then_inc(att_moved, 1)

        @block.vector
        def _(dve):
            x = m.x[:, :, :].rearrange("p (b f t) d -> p b f (t d)", b=B, f=2)
            xt = m.x[:, :, :].rearrange("p (b t) d -> p b t d", b=B)

            def add_bias(b, bias, done, count):
                dve.wait_ge(done, count)
                nc.vector.tensor_tensor(xt[:, b], xt[:, b], bias[:, :].unsqueeze(1).broadcast_to([P, TT, D]), ALU.add).then_inc(done, 1)

            with dve.Fori(0, B) as b:
                ADDS = 3 if moe else 2
                dve.wait_ge(att_made, b + 1)
                for half in (0, 1):
                    nc.vector.tensor_tensor(x[:, b, half, :], x[:, b, half, :], m.psum[:, MADE + half, :], ALU.add).then_inc(att_added, 1)
                if moe:
                    add_bias(b, m.bias_u, att_added, ADDS * b + 2)
                dve.wait_ge(att_added, ADDS * b + ADDS)
                dve.wait_ge(xn_turned, 2 * b)
                normalise(nc, m, dve, b, ln_step, std_ready, xn_ready)
                if not moe:
                    dve.wait_ge(ffn_made, b + 1)
                    for half in (0, 1):
                        nc.vector.tensor_tensor(x[:, b, half, :], x[:, b, half, :], m.psum[:, FFN + half, :], ALU.add).then_inc(ffn_added, 1)
                    add_bias(b, m.bias_ffn, ffn_added, 3 * b + 2)
                else:
                    steps = [0]

                    def step(instruction):
                        steps[0] += 1
                        instruction.then_inc(gate_step, 1)
                        dve.wait_ge(gate_step, GATE_STEPS * b + steps[0])

                    def by_tile(ap):
                        return ap.rearrange("p (t e) -> p t e", e=E)

                    def over(col):
                        return col.unsqueeze(2).broadcast_to([P, TT, E])

                    logits = by_tile(m.psum[:, MADE, 0:TT * E])
                    dve.wait_ge(logits_made, b + 1)
                    step(nc.vector.tensor_reduce(m.gate_col[:, 0, :], logits, axis=AX.X, op=ALU.max))
                    nc.vector.tensor_tensor(by_tile(gate[:, 0, :]), logits, over(m.gate_col[:, 0, :]), ALU.subtract).then_inc(logits_moved, 1)
                    dve.wait_ge(gate_exp, b + 1)
                    step(nc.vector.tensor_reduce(m.gate_col[:, 1, :], by_tile(gate[:, 1, :]), axis=AX.X, op=ALU.add))
                    step(nc.vector.reciprocal(m.gate_col[:, 2, :], m.gate_col[:, 1, :]))
                    step(nc.vector.tensor_tensor(by_tile(gate[:, 2, :]), by_tile(gate[:, 1, :]), over(m.gate_col[:, 2, :]), ALU.mult))
                    one = by_tile(gate[:, 2, :]).unsqueeze(3).broadcast_to([P, TT, E, E])
                    other = by_tile(gate[:, 2, :]).unsqueeze(2).broadcast_to([P, TT, E, E])
                    pairs = [m.gate_pairs[:, n, :, :].rearrange("p (t i) j -> p t i j", i=E) for n in (0, 1)]
                    flat_pairs = [m.gate_pairs[:, n, :, :].rearrange("p (t i) j -> p t (i j)", i=E) for n in (0, 1)]
                    before = m.const[:, C_TIE:C_TIE + E * E].unsqueeze(1).broadcast_to([P, TT, E * E])
                    step(nc.vector.tensor_tensor(pairs[1], other, one, ALU.is_equal))
                    step(nc.vector.tensor_tensor(flat_pairs[1], flat_pairs[1], before, ALU.mult))
                    nc.vector.tensor_tensor(pairs[0], other, one, ALU.is_gt).then_inc(gate_step, 1)
                    steps[0] += 1
                    dve.wait_ge(gate_step, GATE_STEPS * b + steps[0])
                    step(nc.vector.tensor_tensor(flat_pairs[0], flat_pairs[0], flat_pairs[1], ALU.add))
                    step(nc.vector.tensor_reduce(gate[:, 3, :], m.gate_pairs[:, 0, :, :], axis=AX.X, op=ALU.add))
                    assert steps[0] == GATE_STEPS
                    nc.vector.scalar_tensor_tensor(gate[:, 4, :], gate[:, 3, :], 2.0, gate[:, 2, :], ALU.is_lt, ALU.mult).then_inc(gate_ready, 1)
                    dve.wait_ge(gate_ready, b + 1)
                    for e in range(E):
                        dve.wait_ge(expert_made, E * b + e + 1)
                        if e > 0:
                            dve.wait_ge(mixed, E * b + e)
                        bank = 4 + 2 * (e % 2)
                        for t in range(TT):
                            last = nc.vector.scalar_tensor_tensor(
                                xt[:, b, t, :], m.psum[:, bank + t // 4, (t % 4) * P:(t % 4 + 1) * P],
                                gate[:, 4, t * E + e:t * E + e + 1], xt[:, b, t, :], ALU.mult, ALU.add)
                        last.then_inc(mixed, 1)

        @block.sync
        def _(sp):
            if moe:
                with sp.Fori(0, B) as b:
                    sp.wait_ge(mixed, E * (b + 1))
                    sp.dma_start(out.rearrange("b (t p) d -> b p t d", p=P)[b],
                                 m.x[:, :, :].rearrange("p (b t) d -> p b t d", b=B)[:, b]).then_inc(stored, 16)
                sp.wait_ge(stored, 16 * B)


def preln_two_layers(nc, dram, out):
    with ExitStack() as ctx:
        def sem(name):
            return ctx.enter_context(nc.semaphore(name))

        m = Memory(nc, ctx)
        m.passed = sem("passed")
        setup(nc, m, dram, sem)
        for layer in (0, 1):
            prepare(nc, m, layer, sem)
            attention(nc, m, layer, sem)
            finish(nc, m, layer, out, sem)


def constants():
    n = np.arange(P)
    angle = 2.0 * np.pi * ((n[:, None] * n[None, :]) % P) / P
    cos, sin = np.cos(angle), np.sin(angle)
    tri = np.zeros((P, BANK))
    tri[:, BANK - P:] = np.where(n[None, :] > n[:, None], LOW, 0.0)
    head = (n[:, None] // DH == np.arange(HEADS)[None, :])
    e = np.arange(E)
    tie = np.broadcast_to((e[None, :] < e[:, None]).reshape(1, E * E), (P, E * E))
    keep = n[None, :] >= n[:, None]
    return np.concatenate([np.eye(P), cos, sin, -sin, tri, head, tie, keep], axis=1).astype(np.float32)


INPUTS = ["L0_attn_x", "L0_attn_W_qkv", "L0_attn_W_out", "L0_ffn_w_freq_real", "L0_ffn_w_freq_imag", "L0_ffn_bias",
          "L1_attn_Wq", "L1_attn_Wk", "L1_attn_Wv", "L1_attn_Wu", "L1_attn_bu", "L1_ffn_wg1", "L1_ffn_bg1",
          "L1_ffn_wg2", "L1_ffn_w_in", "L1_ffn_w_out"]


def kernel(**inputs):
    import concourse.bacc as bacc
    from concourse.bass_utils import run_bass_kernel_spmd

    nc = bacc.Bacc("TRN2", target_bir_lowering=False, num_devices=1)
    arrays, dram = {}, {}
    for name in INPUTS:
        a = np.ascontiguousarray(inputs[name])
        arrays[f"in_{name}"] = a
        dram[name] = nc.dram_tensor(f"in_{name}", a.shape, mybir.dt.from_np(a.dtype), kind="ExternalInput").ap()
    arrays["in_consts"] = constants()
    dram["consts"] = nc.dram_tensor("in_consts", arrays["in_consts"].shape, FP32, kind="ExternalInput").ap()
    out = nc.dram_tensor("out", (B, T, D), FP32, kind="ExternalOutput").ap()
    preln_two_layers(nc, dram, out)
    result = run_bass_kernel_spmd(nc, [arrays], core_ids=[0])
    return result.results[0]["out"]
```

```python
import numpy as np
import concourse.bass as bass
from concourse import mybir
from contextlib import ExitStack

FP32 = mybir.dt.float32
BF16 = mybir.dt.bfloat16
ALU = mybir.AluOpType
ACT = mybir.ActivationFunctionType
AX = mybir.AxisListType

B, T, D = 4, 1024, 128
HEADS = 16
DH = D // HEADS
P = 128
TT = T // P
NT = B * TT
E, HID, G = 8, 256, 32
HJ = HID // P
EPS = 1e-5
SCALE = (DH ** -0.5, D ** -0.5)

GH = 4
GROUPS = HEADS // GH
Q_PART = (0, 1, 2, 0, 1, 0)
K_PART = (0, 0, 0, 1, 1, 2)
SPLIT = DH * len(Q_PART)
SHIFT = 2
SHIFT_ROW = 96
TWO_ONES = 1.0 + 0x3F80 / 2 ** 23
LOW = -1.0e30

C_ID, C_COS, C_SIN, C_NSIN, C_TRI, C_HEAD, C_TIE, C_END = np.cumsum([0, P, P, P, P, 512, HEADS, 64])

BANK = 512
SCORE_BANKS = 4
OUT_BANK = 4
RING_BANK, RING_DEPTH = 5, 3

SCORE_BANKFULS = [[(4, 0, 0)], [(0, 0, 0), (2, 0, P)], [(5, 0, 0)], [(1, 0, 0), (5, 4, 2 * P)], [(6, 0, 0)],
                  [(3, 0, 0)], [(7, 0, 0)], [(4, 4, 0), (6, 4, P)], [(7, 4, 0)]]
SCORE_FILLS = [(hh, n) for hh in range(GH) for n in range(len(SCORE_BANKFULS))]
NF = len(SCORE_FILLS)
NEXT = 12
SHIFT_AT = 5


def piece_is_full(i, k0):
    return i >= 4 and k0 == 0


def piece_width(i, k0):
    return BANK if piece_is_full(i, k0) else P * (i + 1 - k0)


STEP_UNITS = [
    [[(hh, 0, 0), (hh, 1, 0), (hh, 3, 0)] for hh in range(GH)],
    [[(hh, 2, 0) for hh in range(GH)]],
    [[(hh, 0, 1), (hh, 1, 1)] for hh in range(GH)],
    [[(hh, 2, 1), (hh, 3, 1)] for hh in range(GH)],
    [[(hh, 4, 1), (hh, 5, 1), (hh, 7, 1)] for hh in range(GH)],
    [[(hh, 6, 1) for hh in range(GH)]],
]
STEPS = len(STEP_UNITS)
HALF_END = (1, 5)
UNITS = [len(x) for x in STEP_UNITS]
UNITS_PER_GROUP = sum(UNITS)


def queries(kb, half):
    q0 = max(kb * P, half * BANK)
    return q0, (half + 1) * BANK - q0


def columns(unit):
    out, c = [], 0
    for hh, kb, half in unit:
        out.append((hh, kb, half, c))
        c += queries(kb, half)[1]
    assert c == T, unit
    return out


def unit_number(g, s, u):
    return g * UNITS_PER_GROUP + sum(UNITS[:s]) + u


def prob_slot(s, u):
    return 4 * (s % 2) + u


def value_pieces(s):
    return sorted({(kb, half) for unit in STEP_UNITS[s] for _, kb, half in unit})


def ring_of_groups(b_last):
    out = []
    for g in range(GROUPS):
        here = g + 1 if not (b_last and g + 1 >= GROUPS) else None
        after = g + 2 if not (b_last and g + 2 >= GROUPS) else None
        ring = [("score", here) + f for f in SCORE_FILLS[NEXT:]] if here is not None else []
        n = len(ring)
        ring.insert(3 * n // 4, ("out", g, 0))
        if g > 0:
            ring.insert(n // 3, ("out", g - 1, 1))
        if after is not None:
            ahead = [("score", after) + f for f in SCORE_FILLS[:NEXT]]
            ahead[SHIFT_AT:SHIFT_AT] = [("shift", here)]
        else:
            ahead = [("shift", here)] if here is not None else []
        out.append(ring + ahead)
    return out


def first_ring():
    ahead = [("score", 1) + f for f in SCORE_FILLS[:NEXT]]
    ahead[SHIFT_AT:SHIFT_AT] = [("shift", 0)]
    return [("score", 0) + f for f in SCORE_FILLS] + ahead


def batch_order(last):
    rings = ring_of_groups(last)
    order, pending = [], []
    for g in range(GROUPS):
        main = []
        for s in range(STEPS):
            here = [("unit", g, s, u) for u in range(UNITS[s])]
            n = min(LAG, len(here))
            mixed, rest = here[:n], here[n:]
            for v in pending:
                mixed.append(v)
                if rest:
                    mixed.append(rest.pop(0))
            main += mixed + rest
            pending = [("values", g, s, n) for n in range(len(value_pieces(s)))]
        ring, done = rings[g], 0
        for n, m in enumerate(main):
            order.append(m)
            while (done + 1) * len(main) <= len(ring) * (n + 1):
                order.append(ring[done])
                done += 1
    order += pending
    order += [("out", GROUPS - 1, 1)]
    return order


MASKED_STEPS = (0, 1, 4, 5)


def masked_number(g, s):
    return g * sum(UNITS[x] for x in MASKED_STEPS) + sum(UNITS[x] for x in MASKED_STEPS if x <= s)


LAG = 3
ORDER = {last: batch_order(last) for last in (False, True)}
RING = {last: [x for x in ORDER[last] if x[0] in ("score", "shift", "out")] for last in (False, True)}
FIRST = first_ring()
RING_FIRST = len(FIRST)
RING_BATCH = len(RING[False])
assert RING_BATCH % RING_DEPTH == 0


class Memory:

    def __init__(self, nc, ctx):
        def sb(name, shape, dt=FP32):
            return ctx.enter_context(nc.sbuf_tensor(name, shape, dt))

        self.x = sb("x", [P, NT, D])
        self.const = sb("const", [P, int(C_END)])
        self.ident_bf = sb("ident_bf", [P, P], BF16)
        self.raw = sb("raw", [P, 8, P])
        self.w = sb("w", [P, 9, P])
        self.w8 = sb("w8", [DH, 3, DH])
        self.w8r = sb("w8r", [DH, 3, HEADS, DH])
        self.dft = sb("dft", [P, 2, P])
        self.bias_ffn = sb("bias_ffn", [P, D])
        self.bias_u = sb("bias_u", [P, D])
        self.v = sb("v", [P, NT, D])
        self.att = sb("att", [P, NT, D])
        self.stats = sb("stats", [P, TT, 6])
        self.mv = sb("mv", [P, TT, 2])
        self.std = sb("std", [P, TT])
        self.rstd = sb("rstd", [P, TT])
        self.eps = sb("eps", [P, 1])
        self.q_rows = sb("q_rows", [P, GROUPS, GH, T], BF16)
        self.k_rows = sb("k_rows", [P, GROUPS, GH, T], BF16)
        self.probs = sb("probs", [P, 8, T])
        self.xn = self.probs[:, 0, :].rearrange("p (t d) -> p t d", d=D)
        self.xn_t = self.probs[:, 1, :]
        self.att_b = self.probs[:, 2, :].rearrange("p (t d) -> p t d", d=D)
        self.att_t = self.probs[:, 3, :]
        self.vg = sb("vg", [P, 2, TT, GH, 32])
        self.out_t = sb("out_t", [P, T])
        self.max_a = sb("max_a", [P, 2, GH, TT])
        self.max_b = sb("max_b", [P, 2, GH, TT])
        self.shift = sb("shift", [P, SHIFT, GH, TT], BF16)
        self.shift_t = sb("shift_t", [SHIFT * GH * TT, P], BF16)
        self.scrap = sb("scrap", [P, RING_DEPTH, BANK], BF16)
        self.rden = sb("rden", [P, 2, 4 * GH])
        self.w_in = sb("w_in", [P, E, HID])
        self.w_out = sb("w_out", [P, E, HJ, D])
        self.wg1 = sb("wg1", [P, G])
        self.bg1 = sb("bg1", [G, 1])
        self.wg2 = sb("wg2", [G, E])
        self.gate = sb("gate", [P, 5, TT * E])
        self.gate_pairs = self.raw[:, :, :].rearrange("p n c -> p (n c)").rearrange("p (n i j) -> p n i j", n=2, j=E)
        self.gate_col = sb("gate_col", [P, 3, TT])
        self.psum = ctx.enter_context(nc.psum_tensor("psum", [P, 8, BANK], FP32))
        self.q_dram = nc.dram_tensor("q_split", (HEADS, SPLIT, B * T), BF16, kind="Internal").ap()
        self.k_dram = nc.dram_tensor("k_split", (HEADS, SPLIT, B * T), BF16, kind="Internal").ap()

    def split(self, n):
        return self.probs[:, 5 + n // 2, :].bitcast(BF16)[:, (n % 2) * T:(n % 2 + 1) * T]


Q0, K0, V0, O0, Q1, K1, V1, O1, CIRC = range(9)


def stand(engine, semaphore, value, passed):
    engine.wait_ge(semaphore, value)
    engine.sem_inc(passed, 1)


def setup(nc, m, dram, sem):
    ident = m.const[:, C_ID:C_COS]
    cos, sin, nsin = (m.const[:, c:c + P] for c in (C_COS, C_SIN, C_NSIN))
    loaded, head_loaded, repeated, made, used, half, ready = (
        sem(n) for n in ("setup_loaded", "setup_w8_loaded", "setup_w8_repeated", "setup_psum", "setup_evacuated",
                         "setup_half", "setup_ready"))
    x_loaded, bias_loaded, own = sem("setup_x_loaded"), sem("setup_bias_loaded"), sem("setup_memset")
    with nc.Block() as block:
        @block.sync
        def _(sp):
            sp.dma_start(m.const[:, :], dram["consts"]).then_inc(loaded, 16)
            sp.dma_start(m.raw[:, 0:3, :], dram["L0_attn_W_qkv"].rearrange("(n o) c -> o n c", o=P)).then_inc(loaded, 16)
            sp.dma_start(m.raw[:, 3, :], dram["L0_attn_W_out"]).then_inc(loaded, 16)
            sp.dma_start(m.raw[:, 4, :], dram["L1_attn_Wu"]).then_inc(loaded, 16)
            sp.dma_start(m.raw[:, 5, :], dram["L0_ffn_w_freq_real"]).then_inc(loaded, 16)
            sp.dma_start(m.raw[:, 6, :], dram["L0_ffn_w_freq_imag"]).then_inc(loaded, 16)
            sp.dma_start(m.x[:, :, :], dram["L0_attn_x"].rearrange("b (t p) d -> p (b t) d", p=P)).then_inc(x_loaded, 16)
            sp.dma_start(m.w_in[:, :, :], dram["L1_ffn_w_in"].rearrange("e d h -> d e h")).then_inc(x_loaded, 16)
            sp.dma_start(m.w_out[:, :, :, :], dram["L1_ffn_w_out"].rearrange("e (j h) d -> h e j d", h=P)).then_inc(x_loaded, 16)
            sp.wait_ge(x_loaded, 3 * 16)

        @block.scalar
        def _(act):
            for n, name in enumerate(("L1_attn_Wq", "L1_attn_Wk", "L1_attn_Wv")):
                act.dma_start(m.w8[:, n, :], dram[name]).then_inc(head_loaded, 16)
            act.dma_start(m.bias_ffn[:, :], dram["L0_ffn_bias"].rearrange("(a d) -> a d", a=1).broadcast_to([P, D])).then_inc(bias_loaded, 16)
            act.dma_start(m.bias_u[:, :], dram["L1_attn_bu"].rearrange("(a d) -> a d", a=1).broadcast_to([P, D])).then_inc(bias_loaded, 16)
            act.dma_start(m.wg1[:, :], dram["L1_ffn_wg1"]).then_inc(bias_loaded, 16)
            act.dma_start(m.bg1[:, :], dram["L1_ffn_bg1"].rearrange("(g a) -> g a", a=1)).then_inc(bias_loaded, 16)
            act.dma_start(m.wg2[:, :], dram["L1_ffn_wg2"]).then_inc(bias_loaded, 16)
            act.wait_ge(bias_loaded, 5 * 16)

        @block.gpsimd
        def _(pool):
            k_words = m.k_rows[:, :, :, :].rearrange("p g h t -> p (g h t)").bitcast(FP32)
            nc.gpsimd.memset(k_words[0:SHIFT_ROW, :], 0.0).then_inc(own, 1)
            nc.gpsimd.memset(k_words[SHIFT_ROW:P, :], TWO_ONES).then_inc(own, 1)
            pool.wait_ge(own, 2)
            nc.gpsimd.memset(m.vg[:, :, :, :, :], 0.0).then_inc(own, 1)
            nc.gpsimd.memset(m.eps[:, :], EPS).then_inc(own, 1)
            pool.wait_ge(own, 4)
            nc.gpsimd.memset(m.vg[:, :, :, :, DH:DH + 1], 1.0).then_inc(own, 1)
            pool.wait_ge(own, 5)

        @block.vector
        def _(dve):
            nc.vector.memset(m.q_rows[:, :, :, :].rearrange("p g h t -> p (g h t)").bitcast(FP32), 0.0).then_inc(ready, 1)
            dve.wait_ge(head_loaded, 3 * 16)
            for n in range(3):
                nc.vector.tensor_copy(m.w8r[:, n, :, :], m.w8[:, n, :].unsqueeze(1).broadcast_to([DH, HEADS, DH])).then_inc(repeated, 1)
            dve.wait_ge(loaded, 6 * 16)
            nc.vector.tensor_copy(m.ident_bf[:, :], ident).then_inc(ready, 1)
            dve.wait_ge(made, 1)
            nc.vector.tensor_copy(m.w[:, Q0:O0 + 1, :].rearrange("p a b -> p (a b)"), m.psum[:, 0, :]).then_inc(used, 1)
            dve.wait_ge(made, 2)
            for n in range(3):
                nc.vector.tensor_tensor(
                    m.w[:, Q1 + n, :].rearrange("p (h o) -> p h o", o=DH),
                    m.psum[:, 1, n * DH:(n + 1) * DH].unsqueeze(1).broadcast_to([P, HEADS, DH]),
                    m.const[:, C_HEAD:C_TIE].unsqueeze(2).broadcast_to([P, HEADS, DH]), ALU.mult).then_inc(used, 1)
            nc.vector.tensor_copy(m.w[:, O1, :], m.psum[:, 1, P:2 * P]).then_inc(used, 1)
            dve.wait_ge(made, 3)
            nc.vector.tensor_copy(m.dft[:, :, :].rearrange("p a b -> p (a b)"), m.psum[:, 2, 0:2 * P]).then_inc(half, 1)
            dve.wait_ge(made, 4)
            nc.vector.tensor_scalar(m.w[:, CIRC, :], m.psum[:, 3, 0:P], 1.0 / D, None, ALU.mult).then_inc(used, 1)
            dve.wait_ge(used, 6)
            dve.wait_ge(ready, 2)

        @block.tensor
        def _(pe):
            pe.wait_ge(loaded, 6 * 16)
            for n in range(4):
                last = nc.tensor.transpose(m.psum[:, 0, n * P:(n + 1) * P], m.raw[:, n, :], ident)
            last.then_inc(made, 1)
            pe.wait_ge(repeated, 3)
            for n in range(3):
                nc.tensor.matmul(m.psum[:, 1, n * DH:(n + 1) * DH], m.w8r[:, n, :, :].rearrange("o h c -> o (h c)"),
                                 ident[0:DH, 0:DH], start=True, stop=True)
            nc.tensor.transpose(m.psum[:, 1, P:2 * P], m.raw[:, 4, :], ident).then_inc(made, 1)
            real, imag = m.raw[:, 5, :], m.raw[:, 6, :]
            nc.tensor.matmul(m.psum[:, 2, 0:P], real, cos, start=True, stop=False)
            nc.tensor.matmul(m.psum[:, 2, 0:P], imag, sin, start=False, stop=True)
            nc.tensor.matmul(m.psum[:, 2, P:2 * P], imag, cos, start=True, stop=False)
            nc.tensor.matmul(m.psum[:, 2, P:2 * P], real, nsin, start=False, stop=True).then_inc(made, 1)
            pe.wait_ge(half, 1)
            nc.tensor.matmul(m.psum[:, 3, 0:P], m.dft[:, 0, :], cos, start=True, stop=False)
            nc.tensor.matmul(m.psum[:, 3, 0:P], m.dft[:, 1, :], nsin, start=False, stop=True).then_inc(made, 1)


def deviations(nc, m, act, b, step, std_ready):
    act.wait_ge(step, NORM_STEPS * b + 2 * TT)
    nc.scalar.activation(m.std[:, :], m.mv[:, :, 1], ACT.Sqrt, bias=m.eps[:, :]).then_inc(std_ready, 1)


def normalise(nc, m, dve, b, step, std_ready, xn_ready):
    x = m.x[:, :, :].rearrange("p (b t) d -> p b t d", b=B)
    dve.sem_inc(m.passed, 1)
    for t in range(TT):
        nc.vector.bn_stats(m.stats[:, t, :], x[:, b, t, :]).then_inc(step, 1)
    stand(dve, step, NORM_STEPS * b + TT, m.passed)
    for t in range(TT):
        nc.vector.bn_aggr(m.mv[:, t, :], m.stats[:, t, :]).then_inc(step, 1)
    dve.wait_ge(std_ready, b + 1)
    nc.vector.reciprocal(m.rstd[:, :], m.std[:, :]).then_inc(step, 1)
    dve.wait_ge(step, NORM_STEPS * b + 2 * TT + 1)
    for t in range(TT):
        last = nc.vector.tensor_scalar(m.xn[:, t, :], x[:, b, t, :], m.mv[:, t, 0:1], m.rstd[:, t:t + 1],
                                       ALU.subtract, ALU.mult)
        if t % 4 == 3:
            last.then_inc(xn_ready, 1)


NORM_STEPS = 2 * TT + 1


def transposes(nc, m, pe, src, bank, turned):
    for half in (0, 1):
        for t in range(4):
            last = nc.tensor.transpose(m.psum[:, bank + half, t * P:(t + 1) * P], src(4 * half + t), m.const[:, C_ID:C_COS])
        last.then_inc(turned, 1)


def project_tokens(nc, m, src_t, weight, bank, made):
    for t in range(TT):
        last = nc.tensor.matmul(m.psum[:, bank + t // 4, (t % 4) * P:(t % 4 + 1) * P], src_t[:, t * P:(t + 1) * P],
                                weight, start=True, stop=True)
    last.then_inc(made, 1)


def prepare(nc, m, layer, sem):
    wq, wk, wv = ((Q0, K0, V0), (Q1, K1, V1))[layer]
    names = ("ln_step", "std_ready", "xn_ready", "turned", "xnt_ready", "q_made", "k_made", "v_made", "high_made", "rest_made",
             "middle_made", "low_made", "v_copied", "stored")
    (ln_step, std_ready, xn_ready, turned, xnt_ready, q_made, k_made, v_made, high_made, rest_made, middle_made, low_made,
     v_copied, stored) = (sem(f"prep{layer}_{n}") for n in names)
    STORES = 2 * len(Q_PART) * 16
    scales = (SCALE[layer], 1.0)
    QB, KB, VB = 2, 4, 6
    with nc.Block() as block:
        @block.vector
        def _(dve):
            with dve.Fori(0, B) as b:
                dve.wait_ge(turned, 2 * b)
                normalise(nc, m, dve, b, ln_step, std_ready, xn_ready)
                dve.wait_ge(stored, STORES * b)
                for n, bank in ((0, QB), (1, KB)):
                    dve.wait_ge(high_made, 2 * b + n + 1)
                    nc.vector.scalar_tensor_tensor(m.probs[:, 3 + n, :], m.psum[:, bank:bank + 2, :].rearrange("p a b -> p (a b)"),
                                                   scales[n], m.split(3 * n), ALU.mult, ALU.subtract).then_inc(rest_made, 1)
                for n in (0, 1):
                    dve.wait_ge(rest_made, 2 * b + n + 1)
                    nc.vector.tensor_copy(m.split(3 * n + 1), m.probs[:, 3 + n, :]).then_inc(middle_made, 1)
                for n in (0, 1):
                    dve.wait_ge(middle_made, 2 * b + n + 1)
                    nc.vector.tensor_tensor(m.split(3 * n + 2), m.probs[:, 3 + n, :], m.split(3 * n + 1),
                                            ALU.subtract).then_inc(low_made, 1)

        @block.scalar
        def _(act):
            v = m.v[:, :, :].rearrange("p (b t) d -> p b (t d)", b=B)
            with act.Fori(0, B) as b:
                deviations(nc, m, act, b, ln_step, std_ready)
                act.wait_ge(v_made, b)
                for half in (0, 1):
                    act.wait_ge(turned, 2 * b + half + 1)
                    nc.scalar.activation(m.xn_t[:, half * BANK:(half + 1) * BANK], m.psum[:, half, :], ACT.Copy).then_inc(xnt_ready, 1)
                act.wait_ge(stored, STORES * b)
                for n, bank, made in ((0, QB, q_made), (1, KB, k_made)):
                    act.wait_ge(made, b + 1)
                    nc.scalar.activation(m.split(3 * n), m.psum[:, bank:bank + 2, :].rearrange("p a b -> p (a b)"),
                                         ACT.Copy, scale=scales[n]).then_inc(high_made, 1)
                act.wait_ge(v_made, b + 1)
                nc.scalar.activation(v[:, b, :], m.psum[:, VB:VB + 2, :].rearrange("p a b -> p (a b)"), ACT.Copy).then_inc(v_copied, 1)

        @block.tensor
        def _(pe):
            with pe.Fori(0, B) as b:
                pe.wait_ge(xn_ready, 2 * b + 2)
                transposes(nc, m, pe, lambda t: m.xn[:, t, :], 0, turned)
                pe.wait_ge(xnt_ready, 2 * b + 2)
                pe.wait_ge(rest_made, 2 * b)
                pe.wait_ge(v_copied, b)
                for weight, bank, made in ((wq, QB, q_made), (wk, KB, k_made)):
                    for half in (0, 1):
                        last = nc.tensor.matmul(m.psum[:, bank + half, :], m.w[:, weight, :],
                                                m.xn_t[:, half * BANK:(half + 1) * BANK], start=True, stop=True)
                    last.then_inc(made, 1)
                project_tokens(nc, m, m.xn_t, m.w[:, wv, :], VB, v_made)

        @block.sync
        def _(sp):
            dests = [d.rearrange("h (r d) (b t) -> r b h d t", d=DH, b=B) for d in (m.q_dram, m.k_dram)]
            with sp.Fori(0, B) as b:
                sp.wait_ge(high_made, 2 * b + 2)
                sp.wait_ge(middle_made, 2 * b + 2)
                sp.wait_ge(low_made, 2 * b + 2)
                for n, parts in ((0, Q_PART), (1, K_PART)):
                    for r, part in enumerate(parts):
                        sp.dma_start(dests[n][r, b], m.split(3 * n + part)).then_inc(stored, 16)
            sp.wait_ge(stored, STORES * B)


def attention(nc, m, layer, sem):
    ring_filled, ring_read, shift_ready, shift_loaded = (
        sem(f"att{layer}_{n}") for n in ("ring_filled", "ring_read", "shift_ready", "shift_loaded"))
    rows_loaded = [sem(f"att{layer}_rows_loaded{n}") for n in range(GROUPS)]
    unit_filled, exp_done, masked, values_done, vg_ready, out_copied, den_ready, max_step = (
        sem(f"att{layer}_{n}") for n in ("unit_filled", "exp_done", "masked", "values_done", "vg_ready", "out_copied",
                                         "den_ready", "max_step"))
    UB = GROUPS * UNITS_PER_GROUP
    SB = GROUPS * STEPS
    MB = masked_number(GROUPS, -1)
    LOADS = 2 * 16

    def ring_count(b, n):
        return n if b is None else RING_FIRST + RING_BATCH * b + n

    def ring_bank(b, n):
        return RING_BANK + (n if b is None else RING_FIRST + n) % RING_DEPTH

    def group_count(b, g):
        return g if b is None else GROUPS * b + g

    def over_batches(engine, body):
        with engine.Fori(0, B - 1) as b:
            body(b, False)
        body(B - 1, True)

    with nc.Block() as block:
        @block.sync
        def _(sp):
            def load(g, b):
                for rows, d in ((m.q_rows, m.q_dram), (m.k_rows, m.k_dram)):
                    src = d.rearrange("(g h) r (b t) -> g b r h t", h=GH, b=B)
                    sp.dma_start(rows[0:SPLIT, g % GROUPS, :, :], src[g % GROUPS, b]).then_inc(rows_loaded[g % GROUPS], 16)

            def store_shift(g, copied):
                sp.wait_ge(ring_read, copied)
                dst = m.q_rows[SHIFT_ROW:SHIFT_ROW + SHIFT, g % GROUPS, :, :].rearrange("s h (i t) -> s (h i) t", t=P)
                sp.dma_start(dst, m.shift_t[:, :]).then_inc(shift_loaded, 16)

            load(0, 0)
            load(1, 0)
            store_shift(0, FIRST.index(("shift", 0)) + 1)

            def body(b, last):
                for g in range(GROUPS):
                    if not (last and g + 2 >= GROUPS):
                        sp.wait_ge(unit_filled, UB * b + UNITS_PER_GROUP * g)
                        load(g + 2, b + (g + 2) // GROUPS)
                    if not (last and g + 1 >= GROUPS):
                        store_shift(g + 1, ring_count(b, RING[last].index(("shift", g + 1)) + 1))
            over_batches(sp, body)
            sp.wait_ge(shift_loaded, 16 * B * GROUPS)

        @block.tensor
        def _(pe):
            def fill_ring(item, b, n):
                kind, g = item[0], item[1]
                bank = ring_bank(b, n)
                if not (b is None and n < RING_DEPTH):
                    pe.wait_ge(ring_read, ring_count(b, n) - RING_DEPTH + 1)
                if kind == "score":
                    hh, n_fill = item[2:]
                    buf = g % GROUPS
                    if (hh, n_fill) == (0, 0):
                        pe.wait_ge(rows_loaded[buf], LOADS * ((0 if b is None else b) + g // GROUPS + 1))
                    for i, k0, col in SCORE_BANKFULS[n_fill]:
                        w = piece_width(i, k0)
                        done = nc.tensor.matmul(m.psum[:, bank, col:col + w], m.q_rows[0:SHIFT_ROW, buf, hh, i * P:(i + 1) * P],
                                                m.k_rows[0:SHIFT_ROW, buf, hh, k0 * P:k0 * P + w], start=True, stop=True)
                elif kind == "shift":
                    stand(pe, shift_ready, group_count(b, g) + 1, m.passed)
                    done = nc.tensor.transpose(m.psum[0:64, bank, 0:P // 2].bitcast(BF16),
                                               m.shift[:, :, :, :].rearrange("p s h i -> p (s h i)"), m.ident_bf[:, :])
                else:
                    half = item[2]
                    pe.wait_ge(out_copied, 2 * (GROUPS * b + g) + half + 1)
                    for t in range(4):
                        done = nc.tensor.transpose(m.psum[:, bank, t * P:(t + 1) * P],
                                                   m.out_t[:, half * BANK + t * P:half * BANK + (t + 1) * P], m.const[:, C_ID:C_COS])
                done.then_inc(ring_filled, 1)

            for n, item in enumerate(FIRST):
                fill_ring(item, None, n)

            def body(b, last):
                n_ring = 0
                for item in ORDER[last]:
                    if item[0] == "unit":
                        g, s, u = item[1:]
                        n = unit_number(g, s, u)
                        slot = n % 2
                        if (s, u) == (0, 0):
                            pe.wait_ge(shift_loaded, 16 * (GROUPS * b + g + 1))
                        if isinstance(b, int) or n >= 1:
                            pe.wait_ge(exp_done, UB * b + n - 1)
                        else:
                            pe.wait_ge(exp_done, UB * b)
                        buf = g % GROUPS
                        for hh, kb, half, col in columns(STEP_UNITS[s][u]):
                            q0, width = queries(kb, half)
                            c = col
                            while c < col + width:
                                w = min(col + width, (c // BANK + 1) * BANK) - c
                                q = q0 + c - col
                                done = nc.tensor.matmul(
                                    m.psum[:, 2 * slot + c // BANK, c % BANK:c % BANK + w],
                                    m.k_rows[:, buf, hh, kb * P:(kb + 1) * P],
                                    m.q_rows[:, buf, hh, q:q + w], start=True, stop=True)
                                c += w
                        done.then_inc(unit_filled, 1)
                    elif item[0] == "values":
                        g, s, n = item[1:]
                        kb, half = value_pieces(s)[n]
                        q0, w = queries(kb, half)
                        if n == 0:
                            if s in MASKED_STEPS:
                                pe.wait_ge(masked, MB * b + masked_number(g, s))
                            else:
                                pe.wait_ge(exp_done, UB * b + unit_number(g, s, UNITS[s] - 1) + 1)
                            if s == 0:
                                pe.wait_ge(vg_ready, GROUPS * b + g + 1)
                            if kb == 0:
                                pe.wait_ge(out_copied, 2 * (GROUPS * b + g) + half)
                        for hh in range(GH):
                            u, col = [(u, c) for u, unit in enumerate(STEP_UNITS[s]) for h2, k2, f2, c in columns(unit)
                                      if (h2, k2, f2) == (hh, kb, half)][0]
                            done = nc.tensor.matmul(
                                m.psum[32 * hh:32 * hh + 32, OUT_BANK, q0 % BANK:q0 % BANK + w],
                                m.vg[:, g % 2, kb, hh, :], m.probs[:, prob_slot(s, u), col:col + w],
                                start=(kb == 0), stop=(kb == (2, 6)[half]), tile_position=(0, 32 * hh))
                        if n == len(value_pieces(s)) - 1:
                            done.then_inc(values_done, 1)
                    else:
                        fill_ring(item, b, n_ring)
                        n_ring += 1
            over_batches(pe, body)

        @block.scalar
        def _(act):
            def body(b, last):
                def copy_out(g, half):
                    act.wait_ge(values_done, SB * b + STEPS * g + HALF_END[half] + 1)
                    if g > 0:
                        act.wait_ge(ring_filled, ring_count(b, RING[last].index(("out", g - 1, half)) + 1))
                    nc.scalar.activation(m.out_t[:, half * BANK:(half + 1) * BANK], m.psum[:, OUT_BANK, :], ACT.Copy).then_inc(out_copied, 1)

                for g in range(GROUPS):
                    for s in range(STEPS):
                        for u in range(UNITS[s]):
                            n = unit_number(g, s, u)
                            act.wait_ge(unit_filled, UB * b + n + 1)
                            if u == 0:
                                if isinstance(b, int) or g * STEPS + s >= 2:
                                    act.wait_ge(values_done, SB * b + g * STEPS + s - 1)
                                else:
                                    act.wait_ge(values_done, SB * b)
                            nc.scalar.activation(m.probs[:, prob_slot(s, u), :],
                                                 m.psum[:, 2 * (n % 2):2 * (n % 2) + 2, :].rearrange("p a b -> p (a b)"),
                                                 ACT.Exp).then_inc(exp_done, 1)
                            if (s, u) == (0, LAG - 1) and g > 0:
                                copy_out(g - 1, 1)
                            if (s, u) == (2, LAG - 1):
                                copy_out(g, 0)
                copy_out(GROUPS - 1, 1)
            over_batches(act, body)

        @block.gpsimd
        def _(pool):
            v = m.v[:, :, :].rearrange("p (b t) (g h d) -> p b g t h d", b=B, g=GROUPS, h=GH)

            def lay_values(g, b):
                nc.gpsimd.tensor_copy(m.vg[:, g % 2, :, :, 0:DH], v[:, b + g // GROUPS, g % GROUPS]).then_inc(vg_ready, 1)

            lay_values(0, 0)

            def body(b, last):
                for g in range(GROUPS):
                    for s in range(STEPS):
                        for u, unit in enumerate(STEP_UNITS[s]):
                            tiles = [col for _, kb, half, col in columns(unit) if kb // 4 == half]
                            if not tiles:
                                continue
                            stand(pool, exp_done, UB * b + unit_number(g, s, u) + 1, m.passed)
                            probs = m.probs[:, prob_slot(s, u), :]
                            if len(tiles) == GH:
                                tiled = [probs.rearrange("p (n c) -> p n c", n=GH)[:, :, 0:P]]
                            else:
                                tiled = [probs.rearrange("p (n c) -> p n c", n=2)[:, :, 0:P], probs[:, T - P:T].unsqueeze(1)]
                            assert [n * T // GH for n in range(GH)] == tiles or tiles == [0, BANK, T - P]
                            for tile in tiled:
                                done = nc.gpsimd.affine_select(out=tile, in_=tile, compare_op=ALU.is_ge, fill=0.0, base=0,
                                                               pattern=[[0, tile.shape[1]], [1, P]], channel_multiplier=-1)
                            done.then_inc(masked, 1)
                        if s == 2 and not (last and g + 1 >= GROUPS):
                            pool.wait_ge(values_done, SB * b + STEPS * g)
                            lay_values(g + 1, b)
            over_batches(pool, body)

        @block.vector
        def _(dve):
            def take(item, b, n):
                kind, g = item[0], item[1]
                bank = ring_bank(b, n)
                if kind == "score":
                    hh, n_fill = item[2:]
                    pieces = SCORE_BANKFULS[n_fill]
                    if piece_is_full(*pieces[0][:2]):
                        dve.wait_ge(ring_filled, ring_count(b, n) + 1)
                    else:
                        stand(dve, ring_filled, ring_count(b, n) + 1, m.passed)
                    for i, k0, col in pieces:
                        w = piece_width(i, k0)
                        if piece_is_full(i, k0):
                            done = nc.vector.tensor_reduce(m.max_b[:, g % 2, hh, i:i + 1], m.psum[:, bank, :], axis=AX.X, op=ALU.max)
                        else:
                            done = nc.vector.tensor_tensor_reduce(
                                out=m.scrap[:, bank - RING_BANK, col:col + w], in0=m.psum[:, bank, col:col + w],
                                in1=m.const[:, C_TRI + BANK - w:C_TRI + BANK], scale=1.0, scalar=-3.0e38,
                                op0=ALU.add, op1=ALU.max, accum_out=m.max_a[:, g % 2, hh, i:i + 1])
                    done.then_inc(ring_read, 1)
                    if (hh, n_fill) == SCORE_FILLS[-1]:
                        dve.wait_ge(ring_read, ring_count(b, n) + 1)
                        late = m.max_a[:, g % 2, :, 4:TT]
                        nc.vector.tensor_tensor(late, late, m.max_b[:, g % 2, :, 4:TT], ALU.max).then_inc(max_step, 1)
                        dve.wait_ge(max_step, 2 * group_count(b, g) + 1)
                        flat = m.max_a[:, g % 2, :, :]
                        nc.vector.tensor_scalar(m.shift[:, 0, :, :], flat, -1.0, None, ALU.mult).then_inc(max_step, 1)
                        dve.wait_ge(max_step, 2 * group_count(b, g) + 2)
                        nc.vector.scalar_tensor_tensor(m.shift[:, 1, :, :], flat, -1.0, m.shift[:, 0, :, :],
                                                       ALU.mult, ALU.subtract).then_inc(shift_ready, 1)
                elif kind == "shift":
                    dve.wait_ge(ring_filled, ring_count(b, n) + 1)
                    if b is not None:
                        dve.wait_ge(shift_loaded, 16 * group_count(b, g))
                    nc.vector.tensor_copy(m.shift_t[:, :], m.psum[0:64, bank, 0:P // 2].bitcast(BF16)).then_inc(ring_read, 1)
                else:
                    half = item[2]
                    dve.wait_ge(ring_filled, ring_count(b, n) + 1)
                    att = m.att[:, :, :].rearrange("p (b f t) (g h d) -> p b f g t h d", b=B, f=2, g=GROUPS, h=GH)[:, b, half, g]
                    outs = m.psum[:, bank, :].rearrange("p (t h c) -> p t h c", t=4, h=GH)
                    rden = m.rden[:, half, :].rearrange("p (t h) -> p t h", t=4)
                    nc.vector.reciprocal(rden, outs[:, :, :, DH]).then_inc(den_ready, 1)
                    dve.wait_ge(den_ready, 2 * (GROUPS * b + g) + half + 1)
                    nc.vector.tensor_tensor(att, outs[:, :, :, 0:DH], rden.unsqueeze(3).broadcast_to([P, 4, GH, DH]),
                                            ALU.mult).then_inc(ring_read, 1)

            for n, item in enumerate(FIRST):
                take(item, None, n)

            def body(b, last):
                for n, item in enumerate(RING[last]):
                    take(item, b, n)
            over_batches(dve, body)


def finish(nc, m, layer, out, sem):
    names = ("att_turned", "att_t_ready", "att_made", "att_added", "ln_step", "std_ready", "xn_ready", "xn_turned", "xnt_ready",
             "ffn_made", "ffn_added", "gate_hidden", "gate_gelu", "logits_made", "gate_step", "logits_moved",
             "gate_exp", "gate_ready", "att_moved", "hidden_made", "gelu_done", "expert_made", "mixed", "stored")
    (att_turned, att_t_ready, att_made, att_added, ln_step, std_ready, xn_ready, xn_turned, xnt_ready, ffn_made, ffn_added,
     gate_hidden, gate_gelu, logits_made, gate_step, logits_moved, gate_exp, gate_ready, att_moved, hidden_made, gelu_done,
     expert_made, mixed, stored) = (sem(f"fin{layer}_{n}") for n in names)
    wo = (O0, O1)[layer]
    moe = layer == 1
    ATT_T, MADE, XN_T, FFN = 0, 4, 2, 6
    GELUS = E * HJ
    GATE_STEPS = 9
    gate = m.gate
    gate_g = m.out_t[0:G, :]

    def flat(ap):
        return ap.rearrange("p a b -> p (a b)")

    with nc.Block() as block:
        @block.tensor
        def _(pe):
            with pe.Fori(0, B) as b:
                if moe:
                    pe.wait_ge(gelu_done, GELUS * b)
                    pe.wait_ge(mixed, E * b)
                pe.wait_ge(att_moved, b + 1)
                transposes(nc, m, pe, lambda t: m.att_b[:, t, :], ATT_T, att_turned)
                pe.wait_ge(att_t_ready, 2 * b + 2)
                project_tokens(nc, m, m.att_t, m.w[:, wo, :], MADE, att_made)
                pe.wait_ge(xn_ready, 2 * b + 2)
                transposes(nc, m, pe, lambda t: m.xn[:, t, :], XN_T, xn_turned)
                pe.wait_ge(xnt_ready, 2 * b + 2)
                if not moe:
                    pe.wait_ge(ffn_added, 3 * b)
                    project_tokens(nc, m, m.xn_t, m.w[:, CIRC, :], FFN, ffn_made)
                else:
                    for half in (0, 1):
                        last = nc.tensor.matmul(m.psum[0:G, FFN + half, :], m.wg1[:, :], m.xn_t[:, half * BANK:(half + 1) * BANK],
                                                start=True, stop=True)
                    last.then_inc(gate_hidden, 1)
                    pe.wait_ge(gate_gelu, b + 1)
                    for t in range(TT):
                        last = nc.tensor.matmul(m.psum[:, MADE, t * E:(t + 1) * E], gate_g[:, t * P:(t + 1) * P], m.wg2[:, :],
                                                start=True, stop=True)
                    last.then_inc(logits_made, 1)

                    def hidden(e):
                        for j in range(HJ):
                            if e > 0:
                                pe.wait_ge(gelu_done, GELUS * b + HJ * (e - 1) + j + 1)
                            for half in (0, 1):
                                last = nc.tensor.matmul(m.psum[:, 2 * j + half, :], m.w_in[:, e, j * P:(j + 1) * P],
                                                        m.xn_t[:, half * BANK:(half + 1) * BANK], start=True, stop=True)
                            last.then_inc(hidden_made, 1)

                    def expert(e):
                        bank = 4 + 2 * (e % 2)
                        pe.wait_ge(gelu_done, GELUS * b + HJ * (e + 1))
                        if e == 0:
                            pe.wait_ge(logits_moved, b + 1)
                        elif e >= 2:
                            pe.wait_ge(mixed, E * b + e - 1)
                        for t in range(TT):
                            for j in range(HJ):
                                last = nc.tensor.matmul(m.psum[:, bank + t // 4, (t % 4) * P:(t % 4 + 1) * P],
                                                        m.probs[:, 4 + 2 * (e % 2) + j, t * P:(t + 1) * P], m.w_out[:, e, j, :],
                                                        start=(j == 0), stop=(j == HJ - 1))
                        last.then_inc(expert_made, 1)

                    hidden(0)
                    for e in range(E):
                        if e + 1 < E:
                            hidden(e + 1)
                        expert(e)

        @block.scalar
        def _(act):
            with act.Fori(0, B) as b:
                act.wait_ge(att_made, b)
                for half in (0, 1):
                    act.wait_ge(att_turned, 2 * b + half + 1)
                    nc.scalar.activation(m.att_t[:, half * BANK:(half + 1) * BANK], m.psum[:, ATT_T + half, :], ACT.Copy).then_inc(att_t_ready, 1)
                deviations(nc, m, act, b, ln_step, std_ready)
                if moe:
                    act.wait_ge(expert_made, E * b)
                else:
                    act.wait_ge(ffn_made, b)
                for half in (0, 1):
                    act.wait_ge(xn_turned, 2 * b + half + 1)
                    nc.scalar.activation(m.xn_t[:, half * BANK:(half + 1) * BANK], m.psum[:, XN_T + half, :], ACT.Copy).then_inc(xnt_ready, 1)
                if moe:
                    act.wait_ge(gate_hidden, b + 1)
                    nc.scalar.activation(gate_g, flat(m.psum[0:G, FFN:FFN + 2, :]), ACT.Gelu, bias=m.bg1[:, :]).then_inc(gate_gelu, 1)
                    act.wait_ge(logits_moved, b + 1)
                    nc.scalar.activation(gate[:, 1, :], gate[:, 0, :], ACT.Exp).then_inc(gate_exp, 1)
                    for e in range(E):
                        if e >= 2:
                            act.wait_ge(expert_made, E * b + e - 1)
                        for j in range(HJ):
                            act.wait_ge(hidden_made, GELUS * b + HJ * e + j + 1)
                            nc.scalar.activation(m.probs[:, 4 + 2 * (e % 2) + j, :], flat(m.psum[:, 2 * j:2 * j + 2, :]), ACT.Gelu).then_inc(gelu_done, 1)

        @block.gpsimd
        def _(pool):
            att = m.att[:, :, :].rearrange("p (b t) d -> p b (t d)", b=B)
            with pool.Fori(0, B) as b:
                pool.wait_ge(att_turned, 2 * b)
                nc.gpsimd.tensor_copy(flat(m.att_b[:, :, :]), att[:, b, :]).then_inc(att_moved, 1)

        @block.vector
        def _(dve):
            x = m.x[:, :, :].rearrange("p (b f t) d -> p b f (t d)", b=B, f=2)
            xt = m.x[:, :, :].rearrange("p (b t) d -> p b t d", b=B)

            def add_bias(b, bias, done, count):
                dve.wait_ge(done, count)
                nc.vector.tensor_tensor(xt[:, b], xt[:, b], bias[:, :].unsqueeze(1).broadcast_to([P, TT, D]), ALU.add).then_inc(done, 1)

            with dve.Fori(0, B) as b:
                ADDS = 3 if moe else 2
                dve.wait_ge(att_made, b + 1)
                for half in (0, 1):
                    nc.vector.tensor_tensor(x[:, b, half, :], x[:, b, half, :], m.psum[:, MADE + half, :], ALU.add).then_inc(att_added, 1)
                if moe:
                    add_bias(b, m.bias_u, att_added, ADDS * b + 2)
                dve.wait_ge(att_added, ADDS * b + ADDS)
                dve.wait_ge(xn_turned, 2 * b)
                normalise(nc, m, dve, b, ln_step, std_ready, xn_ready)
                if not moe:
                    dve.wait_ge(ffn_made, b + 1)
                    for half in (0, 1):
                        nc.vector.tensor_tensor(x[:, b, half, :], x[:, b, half, :], m.psum[:, FFN + half, :], ALU.add).then_inc(ffn_added, 1)
                    add_bias(b, m.bias_ffn, ffn_added, 3 * b + 2)
                else:
                    steps = [0]

                    def step(instruction):
                        steps[0] += 1
                        instruction.then_inc(gate_step, 1)
                        dve.wait_ge(gate_step, GATE_STEPS * b + steps[0])

                    def by_tile(ap):
                        return ap.rearrange("p (t e) -> p t e", e=E)

                    def over(col):
                        return col.unsqueeze(2).broadcast_to([P, TT, E])

                    logits = by_tile(m.psum[:, MADE, 0:TT * E])
                    dve.wait_ge(logits_made, b + 1)
                    step(nc.vector.tensor_reduce(m.gate_col[:, 0, :], logits, axis=AX.X, op=ALU.max))
                    nc.vector.tensor_tensor(by_tile(gate[:, 0, :]), logits, over(m.gate_col[:, 0, :]), ALU.subtract).then_inc(logits_moved, 1)
                    dve.wait_ge(gate_exp, b + 1)
                    step(nc.vector.tensor_reduce(m.gate_col[:, 1, :], by_tile(gate[:, 1, :]), axis=AX.X, op=ALU.add))
                    step(nc.vector.reciprocal(m.gate_col[:, 2, :], m.gate_col[:, 1, :]))
                    step(nc.vector.tensor_tensor(by_tile(gate[:, 2, :]), by_tile(gate[:, 1, :]), over(m.gate_col[:, 2, :]), ALU.mult))
                    one = by_tile(gate[:, 2, :]).unsqueeze(3).broadcast_to([P, TT, E, E])
                    other = by_tile(gate[:, 2, :]).unsqueeze(2).broadcast_to([P, TT, E, E])
                    pairs = [m.gate_pairs[:, n, :, :].rearrange("p (t i) j -> p t i j", i=E) for n in (0, 1)]
                    flat_pairs = [m.gate_pairs[:, n, :, :].rearrange("p (t i) j -> p t (i j)", i=E) for n in (0, 1)]
                    before = m.const[:, C_TIE:C_TIE + E * E].unsqueeze(1).broadcast_to([P, TT, E * E])
                    step(nc.vector.tensor_tensor(pairs[1], other, one, ALU.is_equal))
                    step(nc.vector.tensor_tensor(flat_pairs[1], flat_pairs[1], before, ALU.mult))
                    nc.vector.tensor_tensor(pairs[0], other, one, ALU.is_gt).then_inc(gate_step, 1)
                    steps[0] += 1
                    dve.wait_ge(gate_step, GATE_STEPS * b + steps[0])
                    step(nc.vector.tensor_tensor(flat_pairs[0], flat_pairs[0], flat_pairs[1], ALU.add))
                    step(nc.vector.tensor_reduce(gate[:, 3, :], m.gate_pairs[:, 0, :, :], axis=AX.X, op=ALU.add))
                    assert steps[0] == GATE_STEPS
                    nc.vector.scalar_tensor_tensor(gate[:, 4, :], gate[:, 3, :], 2.0, gate[:, 2, :], ALU.is_lt, ALU.mult).then_inc(gate_ready, 1)
                    dve.wait_ge(gate_ready, b + 1)
                    for e in range(E):
                        dve.wait_ge(expert_made, E * b + e + 1)
                        if e > 0:
                            dve.wait_ge(mixed, E * b + e)
                        bank = 4 + 2 * (e % 2)
                        for t in range(TT):
                            last = nc.vector.scalar_tensor_tensor(
                                xt[:, b, t, :], m.psum[:, bank + t // 4, (t % 4) * P:(t % 4 + 1) * P],
                                gate[:, 4, t * E + e:t * E + e + 1], xt[:, b, t, :], ALU.mult, ALU.add)
                        last.then_inc(mixed, 1)

        @block.sync
        def _(sp):
            if moe:
                with sp.Fori(0, B) as b:
                    sp.wait_ge(mixed, E * (b + 1))
                    sp.dma_start(out.rearrange("b (t p) d -> b p t d", p=P)[b],
                                 m.x[:, :, :].rearrange("p (b t) d -> p b t d", b=B)[:, b]).then_inc(stored, 16)
                sp.wait_ge(stored, 16 * B)


def preln_two_layers(nc, dram, out):
    with ExitStack() as ctx:
        def sem(name):
            return ctx.enter_context(nc.semaphore(name))

        m = Memory(nc, ctx)
        m.passed = sem("passed")
        setup(nc, m, dram, sem)
        for layer in (0, 1):
            prepare(nc, m, layer, sem)
            attention(nc, m, layer, sem)
            finish(nc, m, layer, out, sem)


def constants():
    n = np.arange(P)
    angle = 2.0 * np.pi * ((n[:, None] * n[None, :]) % P) / P
    cos, sin = np.cos(angle), np.sin(angle)
    tri = np.zeros((P, BANK))
    tri[:, BANK - P:] = np.where(n[None, :] > n[:, None], LOW, 0.0)
    head = (n[:, None] // DH == np.arange(HEADS)[None, :])
    e = np.arange(E)
    tie = np.broadcast_to((e[None, :] < e[:, None]).reshape(1, E * E), (P, E * E))
    return np.concatenate([np.eye(P), cos, sin, -sin, tri, head, tie], axis=1).astype(np.float32)


INPUTS = ["L0_attn_x", "L0_attn_W_qkv", "L0_attn_W_out", "L0_ffn_w_freq_real", "L0_ffn_w_freq_imag", "L0_ffn_bias",
          "L1_attn_Wq", "L1_attn_Wk", "L1_attn_Wv", "L1_attn_Wu", "L1_attn_bu", "L1_ffn_wg1", "L1_ffn_bg1",
          "L1_ffn_wg2", "L1_ffn_w_in", "L1_ffn_w_out"]


def kernel(**inputs):
    import concourse.bacc as bacc
    from concourse.bass_utils import run_bass_kernel_spmd

    nc = bacc.Bacc("TRN2", target_bir_lowering=False, num_devices=1)
    arrays, dram = {}, {}
    for name in INPUTS:
        a = np.ascontiguousarray(inputs[name])
        arrays[f"in_{name}"] = a
        dram[name] = nc.dram_tensor(f"in_{name}", a.shape, mybir.dt.from_np(a.dtype), kind="ExternalInput").ap()
    arrays["in_consts"] = constants()
    dram["consts"] = nc.dram_tensor("in_consts", arrays["in_consts"].shape, FP32, kind="ExternalInput").ap()
    out = nc.dram_tensor("out", (B, T, D), FP32, kind="ExternalOutput").ap()
    preln_two_layers(nc, dram, out)
    result = run_bass_kernel_spmd(nc, [arrays], core_ids=[0])
    return result.results[0]["out"]
```

```python
import numpy as np
import concourse.bass as bass
from concourse import mybir
from contextlib import ExitStack

FP32 = mybir.dt.float32
BF16 = mybir.dt.bfloat16
ALU = mybir.AluOpType
ACT = mybir.ActivationFunctionType
AX = mybir.AxisListType

B, T, D = 4, 1024, 128
HEADS = 16
DH = D // HEADS
P = 128
TT = T // P
NT = B * TT
E, HID, G = 8, 256, 32
HJ = HID // P
EPS = 1e-5
SCALE = (DH ** -0.5, D ** -0.5)

GH = 4
GROUPS = HEADS // GH
Q_PART = (0, 1, 2, 0, 1, 0)
K_PART = (0, 0, 0, 1, 1, 2)
PARTS = 3
SPLIT = DH * len(Q_PART)
SHIFT = 2
SHIFT_ROW = 96
TWO_ONES = 1.0 + 0x3F80 / 2 ** 23
LOW = -1.0e30

C_ID, C_COS, C_SIN, C_NSIN, C_TRI, C_HEAD, C_TIE, C_END = np.cumsum([0, P, P, P, P, 512, HEADS, 64])

BANK = 512
SCORE_BANKS = 4
OUT_BANK = 4
RING_BANK, RING_DEPTH = 5, 3

SCORE_BANKFULS = [[(4, 0, 0)], [(0, 0, 0), (2, 0, P)], [(5, 0, 0)], [(1, 0, 0), (5, 4, 2 * P)], [(6, 0, 0)],
                  [(3, 0, 0)], [(7, 0, 0)], [(4, 4, 0), (6, 4, P)], [(7, 4, 0)]]
SCORE_FILLS = [(hh, n) for hh in range(GH) for n in range(len(SCORE_BANKFULS))]
NEXT = 11
SHIFT_AT = 5
FIRST_SHIFT_AT = 2


def piece_is_full(i, k0):
    return i >= 4 and k0 == 0


def piece_width(i, k0):
    return BANK if piece_is_full(i, k0) else P * (i + 1 - k0)


STEP_UNITS = [
    [[(hh, 0, 0), (hh, 1, 0), (hh, 3, 0)] for hh in range(GH)],
    [[(hh, 2, 0) for hh in range(GH)]],
    [[(hh, 0, 1), (hh, 1, 1)] for hh in range(GH)],
    [[(hh, 2, 1), (hh, 3, 1)] for hh in range(GH)],
    [[(hh, 4, 1), (hh, 5, 1), (hh, 7, 1)] for hh in range(GH)],
    [[(hh, 6, 1) for hh in range(GH)]],
]
STEPS = len(STEP_UNITS)
HALF_END = (1, 5)
UNITS = [len(x) for x in STEP_UNITS]
UNITS_PER_GROUP = sum(UNITS)


def queries(kb, half):
    q0 = max(kb * P, half * BANK)
    return q0, (half + 1) * BANK - q0


def columns(unit):
    out, c = [], 0
    for hh, kb, half in unit:
        out.append((hh, kb, half, c))
        c += queries(kb, half)[1]
    assert c == T, unit
    return out


def unit_number(g, s, u):
    return g * UNITS_PER_GROUP + sum(UNITS[:s]) + u


FIRST_SLOT = (0, 8, 4, 0, 4, 8)
SLOTS = 9


def prob_slot(s, u):
    return FIRST_SLOT[s] + u


def steps_before_slot(g, s):
    n = g * STEPS + s
    users = [x for x in range(n) if FIRST_SLOT[x % STEPS] == FIRST_SLOT[s]]
    return users[-1] + 1 if users else 0


def value_pieces(s):
    return sorted({(kb, half) for unit in STEP_UNITS[s] for _, kb, half in unit})


def ring_of_group(g, last):
    def exists(group):
        return not last or group < GROUPS

    ring = [("score", g + 1) + f for f in SCORE_FILLS[NEXT:]] if exists(g + 1) else []
    ahead = [("score", g + 2) + f for f in SCORE_FILLS[:NEXT]] if exists(g + 2) else []
    if exists(g + 1):
        ahead = ahead[:SHIFT_AT] + [("shift", g + 1)] + ahead[SHIFT_AT:]
    return ring + ahead


def first_ring():
    ahead = [("score", 1) + f for f in SCORE_FILLS[:NEXT]]
    ahead[FIRST_SHIFT_AT:FIRST_SHIFT_AT] = [("shift", 0)]
    return [("score", 0) + f for f in SCORE_FILLS] + ahead


def cost(item):
    if item[0] == "values":
        return VALUES_COST * queries(*value_pieces(item[2])[item[3]])[1]
    return T if item[0] == "unit" else BANK


def windows(last):
    units = [(g, s, u) for g in range(GROUPS + 1) for s in range(STEPS) for u in range(UNITS[s])]
    behind = [[] for _ in range(len(units) + UNITS_PER_GROUP)]
    position = 0
    for n, (g, s, u) in enumerate(units):
        if not (last and g == GROUPS) and u == UNITS[s] - 1:
            for piece in range(len(value_pieces(s))):
                position = max(position + 1, n + LAG)
                behind[position].append(("values", g, s, piece))
            if s in HALF_END:
                behind[position + OUT_LAG].append(("out", g, HALF_END.index(s)))
    out = []
    for g in range(GROUPS + 1):
        here = range(g * UNITS_PER_GROUP, (g + 1) * UNITS_PER_GROUP)
        main = []
        for n in here:
            if not (last and g == GROUPS):
                main.append(("unit",) + units[n])
            main += behind[n]
        ring = ring_of_group(g, last)
        merged, total, spent, done = [], sum(cost(x) for x in main), 0, 0
        if last and g == GROUPS - 2:
            total *= LAST_RING_SHARE
        for item in main:
            merged.append(item)
            spent += cost(item)
            while done < len(ring) and (done + 1) * total <= len(ring) * spent:
                merged.append(ring[done])
                done += 1
        out.append(merged)
    return out


def split_window(window, g):
    at = window.index(("values", g, 0, 0))
    return window[:at], window[at:]


def renumber(items, groups):
    return [(x[0], x[1] + groups) + x[2:] for x in items if x[1] + groups >= 0]


def batch_order(last):
    w, first_window = windows(last), windows(False)[GROUPS]
    order = renumber(split_window(first_window, GROUPS)[1], -GROUPS) + sum(w[1:GROUPS], [])
    return order + (w[GROUPS] if last else split_window(w[GROUPS], GROUPS)[0])


def first_order():
    return first_ring() + renumber(split_window(windows(False)[GROUPS], GROUPS)[0], -GROUPS)


def copies(order):
    out, units = {}, [x[1:] for x in order if x[0] == "unit"]
    for g in range(GROUPS):
        for half, s in enumerate(HALF_END):
            before = order[:order.index(("values", g, s, len(value_pieces(s)) - 1))]
            n = sum(1 for x in before if x[0] == "unit") - COPY_BACK
            out[g, half] = units[n] if order[-1][0] == "unit" or n < len(units) - COPY_BACK else None
    return out


MASKED_STEPS = (0, 1, 4, 5)


def masked_number(g, s):
    return g * sum(UNITS[x] for x in MASKED_STEPS) + sum(UNITS[x] for x in MASKED_STEPS if x <= s)


LAG = 2
OUT_LAG = 2
COPY_BACK = 1
LAST_RING_SHARE = 0.85
VALUES_COST = 4
ORDER = {last: batch_order(last) for last in (False, True)}
RING = {last: [x for x in ORDER[last] if x[0] in ("score", "shift", "out")] for last in (False, True)}
FIRST = first_order()
FIRST_RING = [x for x in FIRST if x[0] in ("score", "shift")]
COPIES = {last: copies(ORDER[last]) for last in (False, True)}
RING_FIRST = len(FIRST_RING)
RING_BATCH = len(RING[False])
assert RING_BATCH % RING_DEPTH == 0


class Memory:

    def __init__(self, nc, ctx):
        def sb(name, shape, dt=FP32):
            return ctx.enter_context(nc.sbuf_tensor(name, shape, dt))

        self.x = sb("x", [P, NT, D])
        self.const = sb("const", [P, int(C_END)])
        self.ident_bf = sb("ident_bf", [P, P], BF16)
        self.raw = sb("raw", [P, 8, P])
        self.w = sb("w", [P, 9, P])
        self.w8 = sb("w8", [DH, 3, DH])
        self.w8r = sb("w8r", [DH, 3, HEADS, DH])
        self.dft = sb("dft", [P, 2, P])
        self.bias_ffn = sb("bias_ffn", [P, D])
        self.bias_u = sb("bias_u", [P, D])
        self.v = sb("v", [P, NT, D])
        self.att = sb("att", [P, NT, D])
        self.stats = sb("stats", [P, NT, 6])
        self.mv = sb("mv", [P, NT, 2])
        self.std = sb("std", [P, NT])
        self.rstd = sb("rstd", [P, NT])
        self.eps = sb("eps", [P, 1])
        self.q_rows = sb("q_rows", [P, GROUPS, GH, T], BF16)
        self.k_rows = sb("k_rows", [P, GROUPS, GH, T], BF16)
        self.probs = sb("probs", [P, SLOTS, T])
        self.xn2 = self.probs[:, 0:2, :].rearrange("p n (t d) -> p n t d", d=D)
        self.xn2_t = self.probs[:, 2:4, :]
        self.rest = self.probs[:, 4:6, :]
        self.att2 = self.probs[:, 4:6, :].rearrange("p n (t d) -> p n t d", d=D)
        self.att2_t = self.probs[:, 6:8, :]
        self.hidden = self.probs[:, 4:8, :]
        self.gate = self.probs[:, 8, :].rearrange("p (n c) -> p n c", c=NT * E)
        self.gate_pairs = self.probs[:, 0:4, :].rearrange("p n c -> p (n c)").rearrange("p (n i j) -> p n i j", n=2, j=E)
        self.xn_t_all = self.v[:, :, :].rearrange("p (b t) d -> p b (t d)", b=B)
        self.vg = sb("vg", [P, 2, TT, GH, 32])
        self.out_t = sb("out_t", [P, T])
        self.max_a = sb("max_a", [P, 2, GH, TT])
        self.max_b = sb("max_b", [P, 2, GH, TT])
        self.shift = sb("shift", [P, SHIFT, GH, TT], BF16)
        self.shift_t = sb("shift_t", [SHIFT * GH * TT, P], BF16)
        self.scrap = sb("scrap", [P, RING_DEPTH, BANK], BF16)
        self.rden = sb("rden", [P, 2, 4 * GH])
        self.w_in = sb("w_in", [P, E, HID])
        self.w_out = sb("w_out", [P, E, HJ, D])
        self.wg1 = sb("wg1", [P, G])
        self.bg1 = sb("bg1", [G, 1])
        self.wg2 = sb("wg2", [G, E])
        self.gate_col = sb("gate_col", [P, 3, NT])
        self.psum = ctx.enter_context(nc.psum_tensor("psum", [P, 8, BANK], FP32))
        self.q_dram = nc.dram_tensor("q_split", (HEADS, PARTS, DH, B * T), BF16, kind="Internal").ap()
        self.k_dram = nc.dram_tensor("k_split", (HEADS, PARTS, DH, B * T), BF16, kind="Internal").ap()

    def split(self, odd, n):
        att = self.att[:, :, :].rearrange("p (n t) d -> p n (t d)", t=TT)
        slot = 3 * odd + n // 2
        place = att[:, slot, :] if slot < B else self.probs[:, 6 + slot - B, :]
        return place.bitcast(BF16)[:, (n % 2) * T:(n % 2 + 1) * T]


Q0, K0, V0, O0, Q1, K1, V1, O1, CIRC = range(9)


def past(count):
    return count + 1


def stand(engine, semaphore, value, passed):
    engine.wait_ge(semaphore, past(value))
    engine.sem_inc(passed, 1)


PREPARE_SEMAPHORES = ("ln_step", "std_ready", "xn_ready", "turned", "xnt_ready", "q_made", "k_made", "v_made", "high_made",
                      "rest_made", "middle_made", "low_made", "v_copied", "stored")
ATTENTION_SEMAPHORES = ("ring_filled", "ring_read", "shift_ready", "shift_loaded", "rows_loaded0", "rows_loaded1",
                        "rows_loaded2", "rows_loaded3", "unit_filled", "exp_done", "masked", "values_done", "vg_ready",
                        "out_copied", "den_ready", "max_step")
FINISH_SEMAPHORES = ("att_moved", "att_turned", "att_t_ready", "att_made", "att_added", "ln_step", "std_ready", "xn_ready",
                     "xn_turned", "xnt_ready", "ffn_made", "bias_added", "ffn_added", "gate_hidden", "gate_gelu",
                     "logits_made")
EXPERT_SEMAPHORES = ("logits_moved", "gate_exp", "gate_step", "hidden_made", "gelu_done", "expert_made", "mixed", "stored")


def setup(nc, m, dram, sem, phase_semaphores):
    ident = m.const[:, C_ID:C_COS]
    cos, sin, nsin = (m.const[:, c:c + P] for c in (C_COS, C_SIN, C_NSIN))
    loaded, head_loaded, repeated, made, used, half, ready = (
        sem(n) for n in ("setup_loaded", "setup_w8_loaded", "setup_w8_repeated", "setup_psum", "setup_evacuated",
                         "setup_half", "setup_ready"))
    x_loaded, own = sem("setup_x_loaded"), sem("setup_memset")
    with nc.Block() as block:
        @block.sync
        def _(sp):
            sp.dma_start(m.const[:, :], dram["consts"]).then_inc(loaded, 16)
            sp.dma_start(m.raw[:, 0:3, :], dram["L0_attn_W_qkv"].rearrange("(n o) c -> o n c", o=P)).then_inc(loaded, 16)
            sp.dma_start(m.raw[:, 3, :], dram["L0_attn_W_out"]).then_inc(loaded, 16)
            sp.dma_start(m.raw[:, 4, :], dram["L1_attn_Wu"]).then_inc(loaded, 16)
            sp.dma_start(m.raw[:, 5, :], dram["L0_ffn_w_freq_real"]).then_inc(loaded, 16)
            sp.dma_start(m.raw[:, 6, :], dram["L0_ffn_w_freq_imag"]).then_inc(loaded, 16)
            sp.dma_start(m.x[:, :, :], dram["L0_attn_x"].rearrange("b (t p) d -> p (b t) d", p=P)).then_inc(x_loaded, 16)
            for semaphore in phase_semaphores:
                sp.sem_inc(semaphore, 1)
            sp.wait_ge(x_loaded, 16)

        @block.scalar
        def _(act):
            for n, name in enumerate(("L1_attn_Wq", "L1_attn_Wk", "L1_attn_Wv")):
                act.dma_start(m.w8[:, n, :], dram[name]).then_inc(head_loaded, 16)
            act.dma_start(m.bias_ffn[:, :], dram["L0_ffn_bias"].rearrange("(a d) -> a d", a=1).broadcast_to([P, D])).then_inc(m.late_loaded, 16)
            act.dma_start(m.bias_u[:, :], dram["L1_attn_bu"].rearrange("(a d) -> a d", a=1).broadcast_to([P, D])).then_inc(m.late_loaded, 16)
            act.dma_start(m.wg1[:, :], dram["L1_ffn_wg1"]).then_inc(m.late_loaded, 16)
            act.dma_start(m.bg1[:, :], dram["L1_ffn_bg1"].rearrange("(g a) -> g a", a=1)).then_inc(m.late_loaded, 16)
            act.dma_start(m.wg2[:, :], dram["L1_ffn_wg2"]).then_inc(m.late_loaded, 16)

        @block.gpsimd
        def _(pool):
            nc.gpsimd.memset(m.vg[:, :, :, :, :], 0.0).then_inc(own, 1)
            nc.gpsimd.memset(m.eps[:, :], EPS).then_inc(own, 1)
            pool.wait_ge(own, 2)
            nc.gpsimd.memset(m.vg[:, :, :, :, DH:DH + 1], 1.0).then_inc(own, 1)
            pool.wait_ge(own, 3)

        @block.vector
        def _(dve):
            dve.wait_ge(head_loaded, 3 * 16)
            for n in range(3):
                nc.vector.tensor_copy(m.w8r[:, n, :, :], m.w8[:, n, :].unsqueeze(1).broadcast_to([DH, HEADS, DH])).then_inc(repeated, 1)
            dve.wait_ge(loaded, 6 * 16)
            nc.vector.tensor_copy(m.ident_bf[:, :], ident).then_inc(ready, 1)
            dve.wait_ge(made, 1)
            nc.vector.tensor_copy(m.w[:, Q0:O0 + 1, :].rearrange("p a b -> p (a b)"), m.psum[:, 0, :]).then_inc(used, 1)
            dve.wait_ge(made, 2)
            for n in range(3):
                nc.vector.tensor_tensor(
                    m.w[:, Q1 + n, :].rearrange("p (h o) -> p h o", o=DH),
                    m.psum[:, 1, n * DH:(n + 1) * DH].unsqueeze(1).broadcast_to([P, HEADS, DH]),
                    m.const[:, C_HEAD:C_TIE].unsqueeze(2).broadcast_to([P, HEADS, DH]), ALU.mult).then_inc(used, 1)
            nc.vector.tensor_copy(m.w[:, O1, :], m.psum[:, 1, P:2 * P]).then_inc(used, 1)
            dve.wait_ge(made, 3)
            nc.vector.tensor_copy(m.dft[:, :, :].rearrange("p a b -> p (a b)"), m.psum[:, 2, 0:2 * P]).then_inc(half, 1)
            dve.wait_ge(made, 4)
            nc.vector.tensor_scalar(m.w[:, CIRC, :], m.psum[:, 3, 0:P], 1.0 / D, None, ALU.mult).then_inc(used, 1)
            dve.wait_ge(used, 6)
            dve.wait_ge(ready, 1)

        @block.tensor
        def _(pe):
            pe.wait_ge(loaded, 6 * 16)
            for n in range(4):
                last = nc.tensor.transpose(m.psum[:, 0, n * P:(n + 1) * P], m.raw[:, n, :], ident)
            last.then_inc(made, 1)
            pe.wait_ge(repeated, 3)
            for n in range(3):
                nc.tensor.matmul(m.psum[:, 1, n * DH:(n + 1) * DH], m.w8r[:, n, :, :].rearrange("o h c -> o (h c)"),
                                 ident[0:DH, 0:DH], start=True, stop=True)
            nc.tensor.transpose(m.psum[:, 1, P:2 * P], m.raw[:, 4, :], ident).then_inc(made, 1)
            real, imag = m.raw[:, 5, :], m.raw[:, 6, :]
            nc.tensor.matmul(m.psum[:, 2, 0:P], real, cos, start=True, stop=False)
            nc.tensor.matmul(m.psum[:, 2, 0:P], imag, sin, start=False, stop=True)
            nc.tensor.matmul(m.psum[:, 2, P:2 * P], imag, cos, start=True, stop=False)
            nc.tensor.matmul(m.psum[:, 2, P:2 * P], real, nsin, start=False, stop=True).then_inc(made, 1)
            pe.wait_ge(half, 1)
            nc.tensor.matmul(m.psum[:, 3, 0:P], m.dft[:, 0, :], cos, start=True, stop=False)
            nc.tensor.matmul(m.psum[:, 3, 0:P], m.dft[:, 1, :], nsin, start=False, stop=True).then_inc(made, 1)


def statistics(nc, m, t, step):
    nc.vector.bn_stats(m.stats[:, t, :], m.x[:, t, :]).then_inc(step, 1)


PAIR = 2 * TT
LN_STEPS = 2 * PAIR + 1


def deviations(nc, m, act, pair, step, std_ready):
    tiles = slice(pair * PAIR, (pair + 1) * PAIR)
    act.wait_ge(step, past(LN_STEPS * pair + 2 * PAIR))
    nc.scalar.activation(m.std[:, tiles], m.mv[:, tiles, 1], ACT.Sqrt, bias=m.eps[:, :]).then_inc(std_ready, 1)


def normalise(nc, m, dve, pair, step, std_ready, turned, xn_ready):
    tiles = slice(pair * PAIR, (pair + 1) * PAIR)
    stand(dve, step, LN_STEPS * pair + PAIR, m.passed)
    for t in range(pair * PAIR, (pair + 1) * PAIR):
        nc.vector.bn_aggr(m.mv[:, t, :], m.stats[:, t, :]).then_inc(step, 1)
    dve.wait_ge(std_ready, past(pair + 1))
    nc.vector.reciprocal(m.rstd[:, tiles], m.std[:, tiles]).then_inc(step, 1)
    dve.wait_ge(step, past(LN_STEPS * (pair + 1)))
    for b in (2 * pair, 2 * pair + 1):
        if pair > 0:
            dve.wait_ge(turned, past(2 * (b - 1)))
        for t in range(TT):
            n = b * TT + t
            last = nc.vector.tensor_scalar(m.xn2[:, b % 2, t, :], m.x[:, n, :], m.mv[:, n, 0:1], m.rstd[:, n:n + 1],
                                           ALU.subtract, ALU.mult)
        last.then_inc(xn_ready, 1)


def transposes(nc, m, pe, src, bank, turned):
    for half in (0, 1):
        for t in range(4):
            last = nc.tensor.transpose(m.psum[:, bank + half, t * P:(t + 1) * P], src(4 * half + t), m.const[:, C_ID:C_COS])
        last.then_inc(turned, 1)


def project_tokens(nc, m, src_t, weight, bank, made):
    for t in range(TT):
        last = nc.tensor.matmul(m.psum[:, bank + t // 4, (t % 4) * P:(t % 4 + 1) * P], src_t[:, t * P:(t + 1) * P],
                                weight, start=True, stop=True)
    last.then_inc(made, 1)


STORES = 2 * PARTS * 16


def prepare(nc, m, layer, dram, sems, rows_loaded):
    wq, wk, wv = ((Q0, K0, V0), (Q1, K1, V1))[layer]
    (ln_step, std_ready, xn_ready, turned, xnt_ready, q_made, k_made, v_made, high_made, rest_made, middle_made, low_made,
     v_copied, stored) = sems
    scales = (SCALE[layer], 1.0)
    QB, KB, VB = 2, 4, 6
    made = (q_made, k_made)

    def bank_pair(bank):
        return m.psum[:, bank:bank + 2, :].rearrange("p a b -> p (a b)")

    with nc.Block() as block:
        @block.vector
        def _(dve):
            for pair in range(B // 2):
                for t in range(pair * PAIR, (pair + 1) * PAIR):
                    nc.vector.bn_stats(m.stats[:, t, :], m.x[:, t, :]).then_inc(ln_step, 1)
                normalise(nc, m, dve, pair, ln_step, std_ready, turned, xn_ready)
            with dve.Fori(0, B // 2) as i:
                for odd in (0, 1):
                    dve.wait_ge(low_made, past(4 * i + 2 * odd))
                    for n, bank in ((0, QB), (1, KB)):
                        dve.wait_ge(high_made, past(4 * i + 2 * odd + n + 1))
                        nc.vector.scalar_tensor_tensor(m.rest[:, n, :], bank_pair(bank), scales[n], m.split(odd, 3 * n),
                                                       ALU.mult, ALU.subtract).then_inc(rest_made, 1)
                    dve.wait_ge(stored, past(2 * STORES * i))
                    for n in (0, 1):
                        dve.wait_ge(middle_made, past(4 * i + 2 * odd + n + 1))
                        nc.vector.tensor_tensor(m.split(odd, 3 * n + 2), m.rest[:, n, :], m.split(odd, 3 * n + 1),
                                                ALU.subtract).then_inc(low_made, 1)

        @block.scalar
        def _(act):
            v = m.v[:, :, :].rearrange("p (i k t) d -> p i k (t d)", k=2, t=TT)

            def copy_transposes(i):
                act.wait_ge(v_made, past(2 * i))
                for odd in (0, 1):
                    for half in (0, 1):
                        act.wait_ge(turned, past(4 * i + 2 * odd + half + 1))
                        nc.scalar.activation(m.xn2_t[:, odd, half * BANK:(half + 1) * BANK], m.psum[:, half, :],
                                             ACT.Copy).then_inc(xnt_ready, 1)

            def parts(i):
                act.wait_ge(stored, past(2 * STORES * i))
                for odd in (0, 1):
                    for n, bank in ((0, QB), (1, KB)):
                        act.wait_ge(made[n], past(2 * i + odd + 1))
                        nc.scalar.activation(m.split(odd, 3 * n), bank_pair(bank), ACT.Copy, scale=scales[n]).then_inc(high_made, 1)
                    act.wait_ge(v_made, past(2 * i + odd + 1))
                    nc.scalar.activation(v[:, i, odd, :], bank_pair(VB), ACT.Copy).then_inc(v_copied, 1)
                    for n in (0, 1):
                        act.wait_ge(rest_made, past(4 * i + 2 * odd + n + 1))
                        nc.scalar.activation(m.split(odd, 3 * n + 1), m.rest[:, n, :], ACT.Copy).then_inc(middle_made, 1)

            deviations(nc, m, act, 0, ln_step, std_ready)
            copy_transposes(0)
            deviations(nc, m, act, 1, ln_step, std_ready)
            parts(0)
            copy_transposes(1)
            parts(1)

        @block.tensor
        def _(pe):
            with pe.Fori(0, B // 2) as i:
                for odd in (0, 1):
                    pe.wait_ge(xn_ready, past(2 * i + odd + 1))
                    pe.wait_ge(xnt_ready, past(4 * i + 2 * odd))
                    transposes(nc, m, pe, lambda t: m.xn2[:, odd, t, :], 0, turned)
                for odd in (0, 1):
                    pe.wait_ge(xnt_ready, past(4 * i + 2 * odd + 2))
                    for n, weight, bank in ((0, wq, QB), (1, wk, KB)):
                        pe.wait_ge(rest_made, past(4 * i + 2 * odd - 1 + n) if odd else past(4 * i))
                        for half in (0, 1):
                            last = nc.tensor.matmul(m.psum[:, bank + half, :], m.w[:, weight, :],
                                                    m.xn2_t[:, odd, half * BANK:(half + 1) * BANK], start=True, stop=True)
                        last.then_inc(made[n], 1)
                    pe.wait_ge(v_copied, past(2 * i + odd))
                    project_tokens(nc, m, m.xn2_t[:, odd, :], m.w[:, wv, :], VB, v_made)

        @block.gpsimd
        def _(pool):
            if layer == 0:
                q_words, k_words = (rows[:, :, :, :].rearrange("p g h t -> p (g h t)").bitcast(FP32) for rows in (m.q_rows, m.k_rows))
                nc.gpsimd.memset(q_words, 0.0).then_inc(m.rows_set, 1)
                pool.wait_ge(m.rows_set, 1)
                nc.gpsimd.memset(k_words[0:SHIFT_ROW, :], 0.0).then_inc(m.rows_set, 1)
                nc.gpsimd.memset(k_words[SHIFT_ROW:P, :], TWO_ONES).then_inc(m.rows_set, 1)

        @block.sync
        def _(sp):
            if layer == 0:
                sp.dma_start(m.w_in[:, :, :], dram["L1_ffn_w_in"].rearrange("e d h -> d e h")).then_inc(m.late_loaded, 16)
                sp.dma_start(m.w_out[:, :, :, :], dram["L1_ffn_w_out"].rearrange("e (j h) d -> h e j d", h=P)).then_inc(m.late_loaded, 16)
            dests = [d.rearrange("h r d (i k t) -> r i k h d t", k=2, t=T) for d in (m.q_dram, m.k_dram)]
            for i in range(B // 2):
                for odd in (0, 1):
                    for part, part_made in enumerate((high_made, middle_made, low_made)):
                        for n in (0, 1):
                            sp.wait_ge(part_made, past(4 * i + 2 * odd + n + 1))
                            sp.dma_start(dests[n][part, i, odd], m.split(odd, 3 * n + part)).then_inc(stored, 16)
                if i == 0:
                    sp.wait_ge(stored, past(2 * STORES))
                    sp.wait_ge(m.rows_set, 3)
                    for g in (0, 1):
                        load_rows(m, sp, g, 0, rows_loaded)
            if layer == 0:
                sp.wait_ge(m.late_loaded, (2 + 5) * 16)


ROW_LOADS = (3 + len(K_PART)) * 16


def load_rows(m, engine, g, b, rows_loaded):
    src_q, src_k = (d.rearrange("(g h) r d (b t) -> g b r d h t", h=GH, b=B)[g % GROUPS, b] for d in (m.q_dram, m.k_dram))
    for first, count in ((0, 3), (3, 2), (5, 1)):
        engine.dma_start(m.q_rows[first * DH:(first + count) * DH, g % GROUPS, :, :],
                         src_q[0:count].rearrange("r d h t -> (r d) h t")).then_inc(rows_loaded[g % GROUPS], 16)
    for block, part in enumerate(K_PART):
        engine.dma_start(m.k_rows[block * DH:(block + 1) * DH, g % GROUPS, :, :],
                         src_k[part]).then_inc(rows_loaded[g % GROUPS], 16)


def attention(nc, m, layer, sems, stored):
    ring_filled, ring_read, shift_ready, shift_loaded = sems[0:4]
    rows_loaded = sems[4:4 + GROUPS]
    unit_filled, exp_done, masked, values_done, vg_ready, out_copied, den_ready, max_step = sems[4 + GROUPS:]
    UB = GROUPS * UNITS_PER_GROUP
    SB = GROUPS * STEPS
    MB = masked_number(GROUPS, -1)

    def units_of(order):
        return [x[1:] for x in order if x[0] == "unit"]

    def ring_count(b, n):
        return n if b is None else RING_FIRST + RING_BATCH * b + n

    def ring_bank(b, n):
        return RING_BANK + (n if b is None else RING_FIRST + n) % RING_DEPTH

    def group_count(b, g):
        return g if b is None else GROUPS * b + g

    def over_batches(engine, body):
        with engine.Fori(0, B - 1) as b:
            body(b, False)
        body(B - 1, True)

    with nc.Block() as block:
        @block.sync
        def _(sp):
            def store_shift(g, copied):
                sp.wait_ge(ring_read, past(copied))
                dst = m.q_rows[SHIFT_ROW:SHIFT_ROW + SHIFT, g % GROUPS, :, :].rearrange("s h (i t) -> s (h i) t", t=P)
                sp.dma_start(dst, m.shift_t[:, :]).then_inc(shift_loaded, 16)

            sp.wait_ge(stored, past(STORES * B))
            store_shift(0, FIRST_RING.index(("shift", 0)) + 1)

            def body(b, last):
                for g in range(GROUPS):
                    if not (last and g + 2 >= GROUPS):
                        sp.wait_ge(unit_filled, past(UB * b + UNITS_PER_GROUP * g))
                        load_rows(m, sp, g + 2, b + (g + 2) // GROUPS, rows_loaded)
                    if not (last and g + 1 >= GROUPS):
                        store_shift(g + 1, ring_count(b, RING[last].index(("shift", g + 1)) + 1))
            over_batches(sp, body)
            sp.wait_ge(shift_loaded, past(16 * B * GROUPS))

        @block.tensor
        def _(pe):
            def fill_ring(item, b, n):
                kind, g = item[0], item[1]
                bank = ring_bank(b, n)
                if not (b is None and n < RING_DEPTH):
                    pe.wait_ge(ring_read, past(ring_count(b, n) - RING_DEPTH + 1))
                if kind == "score":
                    hh, n_fill = item[2:]
                    buf = g % GROUPS
                    if (hh, n_fill) == (0, 0):
                        pe.wait_ge(rows_loaded[buf], past(ROW_LOADS * ((0 if b is None else b) + g // GROUPS + 1)))
                    for i, k0, col in SCORE_BANKFULS[n_fill]:
                        w = piece_width(i, k0)
                        done = nc.tensor.matmul(m.psum[:, bank, col:col + w], m.q_rows[0:SHIFT_ROW, buf, hh, i * P:(i + 1) * P],
                                                m.k_rows[0:SHIFT_ROW, buf, hh, k0 * P:k0 * P + w], start=True, stop=True)
                elif kind == "shift":
                    stand(pe, shift_ready, group_count(b, g) + 1, m.passed)
                    done = nc.tensor.transpose(m.psum[0:64, bank, 0:P // 2].bitcast(BF16),
                                               m.shift[:, :, :, :].rearrange("p s h i -> p (s h i)"), m.ident_bf[:, :])
                else:
                    half = item[2]
                    pe.wait_ge(out_copied, past(2 * (GROUPS * b + g) + half + 1))
                    for t in range(4):
                        done = nc.tensor.transpose(m.psum[:, bank, t * P:(t + 1) * P],
                                                   m.out_t[:, half * BANK + t * P:half * BANK + (t + 1) * P], m.const[:, C_ID:C_COS])
                done.then_inc(ring_filled, 1)

            def score_unit(item, b):
                g, s, u = item[1:]
                n = unit_number(g, s, u)
                slot = n % 2
                if (s, u) == (0, 0):
                    pe.wait_ge(shift_loaded, past(16 * (GROUPS * b + g + 1)))
                if n >= 2:
                    pe.wait_ge(exp_done, past(UB * b + n - 1))
                buf = g % GROUPS
                for hh, kb, half, col in columns(STEP_UNITS[s][u]):
                    q0, width = queries(kb, half)
                    c = col
                    while c < col + width:
                        w = min(col + width, (c // BANK + 1) * BANK) - c
                        q = q0 + c - col
                        done = nc.tensor.matmul(
                            m.psum[:, 2 * slot + c // BANK, c % BANK:c % BANK + w],
                            m.k_rows[:, buf, hh, kb * P:(kb + 1) * P],
                            m.q_rows[:, buf, hh, q:q + w], start=True, stop=True)
                        c += w
                done.then_inc(unit_filled, 1)

            n_ring = 0
            for item in FIRST:
                if item[0] == "unit":
                    score_unit(item, 0)
                else:
                    fill_ring(item, None, n_ring)
                    n_ring += 1

            def body(b, last):
                n_ring = 0
                for item in ORDER[last]:
                    if item[0] == "unit":
                        score_unit(item, b)
                    elif item[0] == "values":
                        g, s, n = item[1:]
                        kb, half = value_pieces(s)[n]
                        q0, w = queries(kb, half)
                        if n == 0:
                            if s in MASKED_STEPS:
                                pe.wait_ge(masked, past(MB * b + masked_number(g, s)))
                            else:
                                pe.wait_ge(exp_done, past(UB * b + unit_number(g, s, UNITS[s] - 1) + 1))
                            if s == 0:
                                pe.wait_ge(vg_ready, past(GROUPS * b + g + 1))
                            if kb == 0:
                                pe.wait_ge(out_copied, past(2 * (GROUPS * b + g) + half))
                        for hh in range(GH):
                            u, col = [(u, c) for u, unit in enumerate(STEP_UNITS[s]) for h2, k2, f2, c in columns(unit)
                                      if (h2, k2, f2) == (hh, kb, half)][0]
                            done = nc.tensor.matmul(
                                m.psum[32 * hh:32 * hh + 32, OUT_BANK, q0 % BANK:q0 % BANK + w],
                                m.vg[:, g % 2, kb, hh, :], m.probs[:, prob_slot(s, u), col:col + w],
                                start=(kb == 0), stop=(kb == (2, 6)[half]), tile_position=(0, 32 * hh))
                        if n == len(value_pieces(s)) - 1:
                            done.then_inc(values_done, 1)
                    else:
                        fill_ring(item, b, n_ring)
                        n_ring += 1
            over_batches(pe, body)

        @block.scalar
        def _(act):
            def exponential(unit, b):
                g, s, u = unit
                n = unit_number(g, s, u)
                act.wait_ge(unit_filled, past(UB * b + n + 1))
                if u == 0:
                    act.wait_ge(values_done, past(SB * b + steps_before_slot(g, s)))
                nc.scalar.activation(m.probs[:, prob_slot(s, u), :],
                                     m.psum[:, 2 * (n % 2):2 * (n % 2) + 2, :].rearrange("p a b -> p (a b)"),
                                     ACT.Exp).then_inc(exp_done, 1)

            for unit in units_of(FIRST):
                exponential(unit, 0)

            def body(b, last):
                def copy_out(g, half):
                    act.wait_ge(values_done, past(SB * b + STEPS * g + HALF_END[half] + 1))
                    if g > 0:
                        act.wait_ge(ring_filled, past(ring_count(b, RING[last].index(("out", g - 1, half)) + 1)))
                    nc.scalar.activation(m.out_t[:, half * BANK:(half + 1) * BANK], m.psum[:, OUT_BANK, :], ACT.Copy).then_inc(out_copied, 1)

                for unit in units_of(ORDER[last]):
                    exponential(unit, b)
                    for (g, half), after in COPIES[last].items():
                        if after == unit:
                            copy_out(g, half)
                for (g, half), after in COPIES[last].items():
                    if after is None:
                        copy_out(g, half)
            over_batches(act, body)

        @block.gpsimd
        def _(pool):
            v = m.v[:, :, :].rearrange("p (b t) (g h d) -> p b g t h d", b=B, g=GROUPS, h=GH)

            def lay_values(g, b):
                nc.gpsimd.tensor_copy(m.vg[:, g % 2, :, :, 0:DH], v[:, b + g // GROUPS, g % GROUPS]).then_inc(vg_ready, 1)

            lay_values(0, 0)
            if layer == 1:
                nc.gpsimd.tensor_tensor(m.x[:, :, :], m.x[:, :, :], m.bias_u[:, :].unsqueeze(1).broadcast_to([P, NT, D]), ALU.add)

            def mask(unit, b):
                g, s, u = unit
                tiles = [col for _, kb, half, col in columns(STEP_UNITS[s][u]) if kb // 4 == half]
                if not tiles:
                    return
                stand(pool, exp_done, UB * b + unit_number(g, s, u) + 1, m.passed)
                probs = m.probs[:, prob_slot(s, u), :]
                if len(tiles) == GH:
                    tiled = [probs.rearrange("p (n c) -> p n c", n=GH)[:, :, 0:P]]
                else:
                    tiled = [probs.rearrange("p (n c) -> p n c", n=2)[:, :, 0:P], probs[:, T - P:T].unsqueeze(1)]
                assert [n * T // GH for n in range(GH)] == tiles or tiles == [0, BANK, T - P]
                for tile in tiled:
                    done = nc.gpsimd.affine_select(out=tile, in_=tile, compare_op=ALU.is_ge, fill=0.0, base=0,
                                                   pattern=[[0, tile.shape[1]], [1, P]], channel_multiplier=-1)
                done.then_inc(masked, 1)

            for unit in units_of(FIRST):
                mask(unit, 0)

            def body(b, last):
                for unit in units_of(ORDER[last]):
                    mask(unit, b)
                    g = unit[0]
                    if unit[1:] == (3, 0) and not (last and g + 1 >= GROUPS):
                        pool.wait_ge(values_done, past(SB * b + STEPS * g))
                        lay_values(g + 1, b)
            over_batches(pool, body)

        @block.vector
        def _(dve):
            def take(item, b, n):
                kind, g = item[0], item[1]
                bank = ring_bank(b, n)
                if kind == "score":
                    hh, n_fill = item[2:]
                    pieces = SCORE_BANKFULS[n_fill]
                    if piece_is_full(*pieces[0][:2]):
                        dve.wait_ge(ring_filled, past(ring_count(b, n) + 1))
                    else:
                        stand(dve, ring_filled, ring_count(b, n) + 1, m.passed)
                    for i, k0, col in pieces:
                        w = piece_width(i, k0)
                        if piece_is_full(i, k0):
                            done = nc.vector.tensor_reduce(m.max_b[:, g % 2, hh, i:i + 1], m.psum[:, bank, :], axis=AX.X, op=ALU.max)
                        else:
                            done = nc.vector.tensor_tensor_reduce(
                                out=m.scrap[:, bank - RING_BANK, col:col + w], in0=m.psum[:, bank, col:col + w],
                                in1=m.const[:, C_TRI + BANK - w:C_TRI + BANK], scale=1.0, scalar=-3.0e38,
                                op0=ALU.add, op1=ALU.max, accum_out=m.max_a[:, g % 2, hh, i:i + 1])
                    done.then_inc(ring_read, 1)
                    if (hh, n_fill) == SCORE_FILLS[-1]:
                        dve.wait_ge(ring_read, past(ring_count(b, n) + 1))
                        late = m.max_a[:, g % 2, :, 4:TT]
                        nc.vector.tensor_tensor(late, late, m.max_b[:, g % 2, :, 4:TT], ALU.max).then_inc(max_step, 1)
                        dve.wait_ge(max_step, past(2 * group_count(b, g) + 1))
                        flat = m.max_a[:, g % 2, :, :]
                        nc.vector.tensor_scalar(m.shift[:, 0, :, :], flat, -1.0, None, ALU.mult).then_inc(max_step, 1)
                        dve.wait_ge(max_step, past(2 * group_count(b, g) + 2))
                        nc.vector.scalar_tensor_tensor(m.shift[:, 1, :, :], flat, -1.0, m.shift[:, 0, :, :],
                                                       ALU.mult, ALU.subtract).then_inc(shift_ready, 1)
                elif kind == "shift":
                    dve.wait_ge(ring_filled, past(ring_count(b, n) + 1))
                    if b is not None:
                        dve.wait_ge(shift_loaded, past(16 * group_count(b, g)))
                    nc.vector.tensor_copy(m.shift_t[:, :], m.psum[0:64, bank, 0:P // 2].bitcast(BF16)).then_inc(ring_read, 1)
                else:
                    half = item[2]
                    dve.wait_ge(ring_filled, past(ring_count(b, n) + 1))
                    att = m.att[:, :, :].rearrange("p (b f t) (g h d) -> p b f g t h d", b=B, f=2, g=GROUPS, h=GH)[:, b, half, g]
                    outs = m.psum[:, bank, :].rearrange("p (t h c) -> p t h c", t=4, h=GH)
                    rden = m.rden[:, half, :].rearrange("p (t h) -> p t h", t=4)
                    nc.vector.reciprocal(rden, outs[:, :, :, DH]).then_inc(den_ready, 1)
                    dve.wait_ge(den_ready, past(2 * (GROUPS * b + g) + half + 1))
                    nc.vector.tensor_tensor(att, outs[:, :, :, 0:DH], rden.unsqueeze(3).broadcast_to([P, 4, GH, DH]),
                                            ALU.mult).then_inc(ring_read, 1)

            for n, item in enumerate(FIRST_RING):
                take(item, None, n)

            def body(b, last):
                for n, item in enumerate(RING[last]):
                    take(item, b, n)
            over_batches(dve, body)


def finish(nc, m, layer, sems):
    (att_moved, att_turned, att_t_ready, att_made, att_added, ln_step, std_ready, xn_ready, xn_turned, xnt_ready, ffn_made,
     bias_added, ffn_added, gate_hidden, gate_gelu, logits_made) = sems
    wo = (O0, O1)[layer]
    moe = layer == 1
    TURNED, MADE = (0, 2), (4, 6)
    HIDDEN = (6, TURNED[1])
    gate_g = m.xn2_t[0:G, :, :]
    x = m.x[:, :, :].rearrange("p (b f t) d -> p b f (t d)", b=B, f=2)

    with nc.Block() as block:
        @block.tensor
        def _(pe):
            with pe.Fori(0, B // 2) as i:
                for odd in (0, 1):
                    pe.wait_ge(att_moved, past(2 * i + odd + 1))
                    pe.wait_ge(att_t_ready, past(4 * i))
                    transposes(nc, m, pe, lambda t: m.att2[:, odd, t, :], TURNED[odd], att_turned)
                for odd in (0, 1):
                    pe.wait_ge(att_t_ready, past(4 * i + 2 * odd + 2))
                    pe.wait_ge(att_added, past(4 * i))
                    project_tokens(nc, m, m.att2_t[:, odd, :], m.w[:, wo, :], MADE[odd], att_made)
            logits = m.psum[:, LOGITS, 0:NT * E].rearrange("p (i k t e) -> p i k t e", k=2, t=TT, e=E)
            with pe.Fori(0, B // 2) as i:
                if moe:
                    pe.wait_ge(gate_gelu, past(2 * i))
                for odd in (0, 1):
                    pe.wait_ge(xn_ready, past(2 * i + odd + 1))
                    pe.wait_ge(xnt_ready, past(4 * i))
                    transposes(nc, m, pe, lambda t: m.xn2[:, odd, t, :], TURNED[odd], xn_turned)
                pe.wait_ge(att_added, past(2 * B))
                if not moe:
                    for odd in (0, 1):
                        pe.wait_ge(xnt_ready, past(4 * i + 2 * odd + 2))
                        pe.wait_ge(ffn_added, past(4 * i))
                        project_tokens(nc, m, m.xn2_t[:, odd, :], m.w[:, CIRC, :], MADE[odd], ffn_made)
                else:
                    xn_t = m.xn_t_all.rearrange("p (i k) c -> p i k c", k=2)
                    pe.wait_ge(xnt_ready, past(4 * i + 4))
                    for odd in (0, 1):
                        for half in (0, 1):
                            last = nc.tensor.matmul(m.psum[0:G, HIDDEN[odd] + half, :], m.wg1[:, :],
                                                    xn_t[:, i, odd, half * BANK:(half + 1) * BANK], start=True, stop=True)
                        last.then_inc(gate_hidden, 1)
                    for odd in (0, 1):
                        pe.wait_ge(gate_gelu, past(2 * i + odd + 1))
                        for t in range(TT):
                            last = nc.tensor.matmul(logits[:, i, odd, t, :], gate_g[:, odd, t * P:(t + 1) * P], m.wg2[:, :],
                                                    start=True, stop=True)
                        last.then_inc(logits_made, 1)

        @block.scalar
        def _(act):
            def copy_transposes(i, to, turned, ready):
                for odd in (0, 1):
                    for half in (0, 1):
                        act.wait_ge(turned, past(4 * i + 2 * odd + half + 1))
                        nc.scalar.activation(to(odd)[:, half * BANK:(half + 1) * BANK], m.psum[:, TURNED[odd] + half, :],
                                             ACT.Copy).then_inc(ready, 1)

            with act.Fori(0, B // 2) as i:
                act.wait_ge(att_made, past(2 * i))
                copy_transposes(i, lambda odd: m.att2_t[:, odd, :], att_turned, att_t_ready)
            deviations(nc, m, act, 0, ln_step, std_ready)
            for i in range(B // 2):
                if not moe:
                    act.wait_ge(ffn_made, past(2 * i))
                    copy_transposes(i, lambda odd: m.xn2_t[:, odd, :], xn_turned, xnt_ready)
                else:
                    copy_transposes(i, lambda odd: m.xn_t_all[:, 2 * i + odd, :], xn_turned, xnt_ready)
                if i == 0:
                    deviations(nc, m, act, 1, ln_step, std_ready)
                if moe:
                    for odd in (0, 1):
                        act.wait_ge(gate_hidden, past(2 * i + odd + 1))
                        act.wait_ge(logits_made, past(2 * i))
                        nc.scalar.activation(gate_g[:, odd, :], m.psum[0:G, HIDDEN[odd]:HIDDEN[odd] + 2, :].rearrange("p a b -> p (a b)"),
                                             ACT.Gelu, bias=m.bg1[:, :]).then_inc(gate_gelu, 1)

        @block.gpsimd
        def _(pool):
            if not moe:
                for b in range(B):
                    pool.wait_ge(xn_ready, past(b + 1))
                    tokens = m.x[:, b * TT:(b + 1) * TT, :]
                    nc.gpsimd.tensor_tensor(tokens, tokens, m.bias_ffn[:, :].unsqueeze(1).broadcast_to([P, TT, D]),
                                            ALU.add).then_inc(bias_added, 1)

        @block.vector
        def _(dve):
            for b in range(B):
                if b >= 2:
                    dve.wait_ge(att_turned, past(2 * (b - 1)))
                nc.vector.tensor_copy(m.att2[:, b % 2, :, :], m.att[:, b * TT:(b + 1) * TT, :]).then_inc(att_moved, 1)
            for pair in range(B // 2):
                for b in (2 * pair, 2 * pair + 1):
                    dve.wait_ge(att_made, past(b + 1))
                    for half in (0, 1):
                        nc.vector.tensor_tensor(x[:, b, half, :], x[:, b, half, :], m.psum[:, MADE[b % 2] + half, :],
                                                ALU.add).then_inc(att_added, 1)
                    stand(dve, att_added, 2 * b + 2, m.passed)
                    for t in range(b * TT, (b + 1) * TT):
                        nc.vector.bn_stats(m.stats[:, t, :], m.x[:, t, :]).then_inc(ln_step, 1)
                normalise(nc, m, dve, pair, ln_step, std_ready, xn_turned, xn_ready)
            if not moe:
                for b in range(B):
                    dve.wait_ge(ffn_made, past(b + 1))
                    dve.wait_ge(bias_added, past(b + 1))
                    for half in (0, 1):
                        nc.vector.tensor_tensor(x[:, b, half, :], x[:, b, half, :], m.psum[:, MADE[b % 2] + half, :],
                                                ALU.add).then_inc(ffn_added, 1)


LOGITS = 4


def experts(nc, m, out, sems):
    logits_moved, gate_exp, gate_step, hidden_made, gelu_done, expert_made, mixed, stored = sems
    GELUS = E * HJ
    gate = m.gate

    def over_batches(engine, body):
        with engine.Fori(0, B - 1) as b:
            body(b, False)
        body(B - 1, True)

    with nc.Block() as block:
        @block.tensor
        def _(pe):
            def hidden(b, e):
                for j in range(HJ):
                    if e > 0:
                        pe.wait_ge(gelu_done, past(GELUS * b + HJ * (e - 1) + j + 1))
                    for half in (0, 1):
                        last = nc.tensor.matmul(m.psum[:, 2 * j + half, :], m.w_in[:, e % E, j * P:(j + 1) * P],
                                                m.xn_t_all[:, b + e // E, half * BANK:(half + 1) * BANK], start=True, stop=True)
                    last.then_inc(hidden_made, 1)

            def expert(b, e):
                bank = 4 + 2 * (e % 2)
                pe.wait_ge(gelu_done, past(GELUS * b + HJ * (e + 1)))
                pe.wait_ge(logits_moved, past(1))
                pe.wait_ge(mixed, past(E * b + e))
                for t in range(TT):
                    for j in range(HJ):
                        last = nc.tensor.matmul(m.psum[:, bank + t // 4, (t % 4) * P:(t % 4 + 1) * P],
                                                m.hidden[:, 2 * (e % 2) + j, t * P:(t + 1) * P], m.w_out[:, e, j, :],
                                                start=(j == 0), stop=(j == HJ - 1))
                last.then_inc(expert_made, 1)

            hidden(0, 0)

            def body(b, last):
                for e in range(E):
                    if not (last and e == E - 1):
                        hidden(b, e + 1)
                    expert(b, e)
            over_batches(pe, body)

        @block.scalar
        def _(act):
            def gelu(b, e):
                for j in range(HJ):
                    act.wait_ge(hidden_made, past(GELUS * b + HJ * e + j + 1))
                    if e > 0:
                        act.wait_ge(expert_made, past(E * b + e - 1))
                    nc.scalar.activation(m.hidden[:, 2 * (e % 2) + j, :], m.psum[:, 2 * j:2 * j + 2, :].rearrange("p a b -> p (a b)"),
                                         ACT.Gelu).then_inc(gelu_done, 1)

            act.wait_ge(logits_moved, past(1))
            nc.scalar.activation(gate[:, 1, :], gate[:, 0, :], ACT.Exp).then_inc(gate_exp, 1)
            gelu(0, 0)

            def body(b, last):
                for e in range(E):
                    if not (last and e == E - 1):
                        gelu(b, e + 1)
            over_batches(act, body)

        @block.vector
        def _(dve):
            xt = m.x[:, :, :].rearrange("p (b t) d -> p b t d", b=B)
            top = gate[:, 3, :].rearrange("p (b t e) -> p b t e", b=B, e=E)
            steps = [0]

            def step(instruction):
                steps[0] += 1
                instruction.then_inc(gate_step, 1)
                dve.wait_ge(gate_step, past(steps[0]))

            def by_tile(ap):
                return ap.rearrange("p (t e) -> p t e", e=E)

            def over(col):
                return col.unsqueeze(2).broadcast_to([P, NT, E])

            logits = by_tile(m.psum[:, LOGITS, 0:NT * E])
            step(nc.vector.tensor_reduce(m.gate_col[:, 0, :], logits, axis=AX.X, op=ALU.max))
            nc.vector.tensor_tensor(by_tile(gate[:, 0, :]), logits, over(m.gate_col[:, 0, :]), ALU.subtract).then_inc(logits_moved, 1)
            dve.wait_ge(gate_exp, past(1))
            step(nc.vector.tensor_reduce(m.gate_col[:, 1, :], by_tile(gate[:, 1, :]), axis=AX.X, op=ALU.add))
            step(nc.vector.reciprocal(m.gate_col[:, 2, :], m.gate_col[:, 1, :]))
            step(nc.vector.tensor_tensor(by_tile(gate[:, 2, :]), by_tile(gate[:, 1, :]), over(m.gate_col[:, 2, :]), ALU.mult))
            one = by_tile(gate[:, 2, :]).unsqueeze(3).broadcast_to([P, NT, E, E])
            other = by_tile(gate[:, 2, :]).unsqueeze(2).broadcast_to([P, NT, E, E])
            pairs = [m.gate_pairs[:, n, :, :].rearrange("p (t i) j -> p t i j", i=E) for n in (0, 1)]
            flat_pairs = [m.gate_pairs[:, n, :, :].rearrange("p (t i) j -> p t (i j)", i=E) for n in (0, 1)]
            before = m.const[:, C_TIE:C_TIE + E * E].unsqueeze(1).broadcast_to([P, NT, E * E])
            nc.vector.tensor_tensor(pairs[0], other, one, ALU.is_gt).then_inc(gate_step, 1)
            steps[0] += 1
            step(nc.vector.tensor_tensor(pairs[1], other, one, ALU.is_equal))
            step(nc.vector.tensor_tensor(flat_pairs[1], flat_pairs[1], before, ALU.mult))
            step(nc.vector.tensor_tensor(flat_pairs[0], flat_pairs[0], flat_pairs[1], ALU.add))
            step(nc.vector.tensor_reduce(gate[:, 0, :], m.gate_pairs[:, 0, :, :], axis=AX.X, op=ALU.add))
            nc.vector.scalar_tensor_tensor(gate[:, 3, :], gate[:, 0, :], 2.0, gate[:, 2, :], ALU.is_lt, ALU.mult).then_inc(mixed, 1)
            with dve.Fori(0, B) as b:
                for e in range(E):
                    dve.wait_ge(expert_made, past(E * b + e + 1))
                    dve.wait_ge(mixed, past(E * b + e + 1))
                    bank = 4 + 2 * (e % 2)
                    for t in range(TT):
                        last = nc.vector.scalar_tensor_tensor(
                            xt[:, b, t, :], m.psum[:, bank + t // 4, (t % 4) * P:(t % 4 + 1) * P],
                            top[:, b, t, e:e + 1], xt[:, b, t, :], ALU.mult, ALU.add)
                    last.then_inc(mixed, 1)

        @block.sync
        def _(sp):
            with sp.Fori(0, B) as b:
                sp.wait_ge(mixed, past(E * b + E + 1))
                sp.dma_start(out.rearrange("b (t p) d -> b p t d", p=P)[b],
                             m.x[:, :, :].rearrange("p (b t) d -> p b t d", b=B)[:, b]).then_inc(stored, 16)
            sp.wait_ge(stored, past(16 * B))


def preln_two_layers(nc, dram, out):
    with ExitStack() as ctx:
        def sem(name):
            return ctx.enter_context(nc.semaphore(name))

        m = Memory(nc, ctx)
        m.passed = sem("passed")
        m.late_loaded = sem("late_loaded")
        m.rows_set = sem("rows_set")
        prep, att, fin = ([[sem(f"{kind}{layer}_{name}") for name in names] for layer in (0, 1)] for kind, names in
                          (("prep", PREPARE_SEMAPHORES), ("att", ATTENTION_SEMAPHORES), ("fin", FINISH_SEMAPHORES)))
        moe = [sem(f"moe_{name}") for name in EXPERT_SEMAPHORES]
        rows_loaded = [att[layer][4:4 + GROUPS] for layer in (0, 1)]
        setup(nc, m, dram, sem, [semaphore for phase in prep + att + fin + [moe] for semaphore in phase])
        for layer in (0, 1):
            prepare(nc, m, layer, dram, prep[layer], rows_loaded[layer])
            attention(nc, m, layer, att[layer], prep[layer][-1])
            finish(nc, m, layer, fin[layer])
        experts(nc, m, out, moe)


def constants():
    n = np.arange(P)
    angle = 2.0 * np.pi * ((n[:, None] * n[None, :]) % P) / P
    cos, sin = np.cos(angle), np.sin(angle)
    tri = np.zeros((P, BANK))
    tri[:, BANK - P:] = np.where(n[None, :] > n[:, None], LOW, 0.0)
    head = (n[:, None] // DH == np.arange(HEADS)[None, :])
    e = np.arange(E)
    tie = np.broadcast_to((e[None, :] < e[:, None]).reshape(1, E * E), (P, E * E))
    return np.concatenate([np.eye(P), cos, sin, -sin, tri, head, tie], axis=1).astype(np.float32)


INPUTS = ["L0_attn_x", "L0_attn_W_qkv", "L0_attn_W_out", "L0_ffn_w_freq_real", "L0_ffn_w_freq_imag", "L0_ffn_bias",
          "L1_attn_Wq", "L1_attn_Wk", "L1_attn_Wv", "L1_attn_Wu", "L1_attn_bu", "L1_ffn_wg1", "L1_ffn_bg1",
          "L1_ffn_wg2", "L1_ffn_w_in", "L1_ffn_w_out"]


def kernel(**inputs):
    import concourse.bacc as bacc
    from concourse.bass_utils import run_bass_kernel_spmd

    nc = bacc.Bacc("TRN2", target_bir_lowering=False, num_devices=1)
    arrays, dram = {}, {}
    for name in INPUTS:
        a = np.ascontiguousarray(inputs[name])
        arrays[f"in_{name}"] = a
        dram[name] = nc.dram_tensor(f"in_{name}", a.shape, mybir.dt.from_np(a.dtype), kind="ExternalInput").ap()
    arrays["in_consts"] = constants()
    dram["consts"] = nc.dram_tensor("in_consts", arrays["in_consts"].shape, FP32, kind="ExternalInput").ap()
    out = nc.dram_tensor("out", (B, T, D), FP32, kind="ExternalOutput").ap()
    preln_two_layers(nc, dram, out)
    result = run_bass_kernel_spmd(nc, [arrays], core_ids=[0])
    return result.results[0]["out"]
```
